# Optimizing a Trainium2 kernel written in Bass

```python
import numpy as np
import jax
import jax.numpy as jnp

def _softmax(x, axis=-1):
    return jax.nn.softmax(x, axis=axis)

def _gelu(x):
    return jax.nn.gelu(x, approximate=True)

def _silu(x):
    return jax.nn.silu(x)

def _sigmoid(x):
    return jax.nn.sigmoid(x)

def _layernorm(x, axis=-1, eps=1e-05):
    m = jnp.mean(x, axis=axis, keepdims=True)
    v = jnp.var(x, axis=axis, keepdims=True)
    return (x - m) / jnp.sqrt(v + eps)

def _scatter_add(tgt, idx, src, axis=0):
    return tgt.at[idx].add(src)

def _segment_sum(src, seg, n):
    return jax.ops.segment_sum(src, seg, n)
kernel_name = 'mk_gnn_resnorm_d4_gnn_r8_a47b42'

def setup_inputs(seed: int=0):
    np.random.seed(seed)
    _w = jnp.asarray

    def _rec_inputs():
        import jax
        import jax.numpy as jnp
        _gk = jax.random.key(seed)
        x = -0.0001006 + 1 * jax.random.normal(jax.random.fold_in(_gk, 1), (6250, 96), jnp.float32)
        _s = jax.random.randint(jax.random.fold_in(_gk, 2), (50000,), 0, 6250, jnp.int32)
        _d = jax.random.randint(jax.random.fold_in(_gk, 3), (50000,), 0, 6250, jnp.int32)
        _loop = jnp.arange(6250, dtype=jnp.int32)
        src = jnp.concatenate([_s, _d, _loop])
        dst = jnp.concatenate([_d, _s, _loop])
        _o = jnp.argsort(dst, stable=True)
        src = src[_o]
        dst = dst[_o]
        edge_attr_17 = jax.random.uniform(jax.random.fold_in(_gk, 12), (106250, 17), jnp.float32, 0.0, 1)
        edge_attr_32 = 0.000196303 + 1.00016 * jax.random.normal(jax.random.fold_in(_gk, 13), (106250, 32), jnp.float32)
        return (x, src, dst, edge_attr_17, edge_attr_32)
    x, src, dst, edge_attr_17, edge_attr_32 = _rec_inputs()

    def _L0_gnn_setup():
        import jax, jax.numpy as jnp
        import numpy as np
        N, E = (6250, 100000)
        DIN = DOUT = 96
        DE = 32

        def _egnn_conv(x, src, dst, edge_attr, W_msg, W_edge, W_root, b):
            msg = x[src] @ W_msg + edge_attr @ W_edge
            agg = jax.ops.segment_max(msg, dst, num_segments=x.shape[0])
            agg = jnp.where(jnp.isneginf(agg), 0.0, agg)
            return agg + x @ W_root + b
        key = jax.random.key(seed)
        ks = jax.random.split(key, 10)
        rn = lambda k, sh, sc: jax.random.normal(k, sh, jnp.float32) * sc
        return {'X': rn(ks[0], (N, DIN), 1.0), 'edge_index': jax.random.randint(ks[1], (2, E), 0, N, jnp.int32), 'edge_attr': rn(ks[2], (E, DE), 1.0), 'W1_msg': rn(ks[3], (DIN, DOUT), DIN ** (-0.5)), 'W1_edge': rn(ks[4], (DE, DOUT), DE ** (-0.5)), 'W1_root': rn(ks[5], (DIN, DOUT), DIN ** (-0.5)), 'b1': jnp.zeros((DOUT,), jnp.float32), 'W2_msg': rn(ks[6], (DOUT, DOUT), DOUT ** (-0.5)), 'W2_edge': rn(ks[7], (DE, DOUT), DE ** (-0.5)), 'W2_root': rn(ks[8], (DOUT, DOUT), DOUT ** (-0.5)), 'b2': jnp.zeros((DOUT,), jnp.float32)}
    _L0_gnn_all = _L0_gnn_setup()
    _L0_gnn_in = {k: v for k, v in _L0_gnn_all.items() if k in ('W1_msg', 'W1_edge', 'W1_root', 'b1', 'W2_msg', 'W2_edge', 'W2_root', 'b2')}
    del _L0_gnn_all

    def _L1_gnn_setup():
        import jax, jax.numpy as jnp
        import numpy as np
        N = 6250
        E = 100000
        D = 96
        ED = 17
        key = jax.random.key(seed)
        ks = jax.random.split(key, 12)
        x = jax.random.normal(ks[0], (N, D), dtype=jnp.float32)
        edge_index = jax.random.randint(ks[1], (2, E), 0, N, dtype=jnp.int64)
        edge_attr = jax.random.uniform(ks[2], (E, ED), dtype=jnp.float32)
        s = 1.0 / np.sqrt(ED)
        W1 = jax.random.uniform(ks[3], (D, ED), jnp.float32, -s, s)
        b1 = jax.random.uniform(ks[4], (D,), jnp.float32, -s, s)
        s = 1.0 / np.sqrt(D)
        W2 = jax.random.uniform(ks[5], (D, D), jnp.float32, -s, s)
        b2 = jax.random.uniform(ks[6], (D,), jnp.float32, -s, s)
        Ws = jax.random.uniform(ks[7], (D, D), jnp.float32, -s, s)
        bs = jax.random.uniform(ks[8], (D,), jnp.float32, -s, s)
        Wn = jax.random.uniform(ks[9], (D, D), jnp.float32, -s, s)
        bn = jax.random.uniform(ks[10], (D,), jnp.float32, -s, s)
        return {'x': x, 'edge_index': edge_index, 'edge_attr': edge_attr, 'W1': W1, 'b1': b1, 'W2': W2, 'b2': b2, 'Ws': Ws, 'bs': bs, 'Wn': Wn, 'bn': bn}
    _L1_gnn_all = _L1_gnn_setup()
    _L1_gnn_in = {k: v for k, v in _L1_gnn_all.items() if k in ('W1', 'b1', 'W2', 'b2', 'Ws', 'bs', 'Wn', 'bn')}
    del _L1_gnn_all

    def _L2_gnn_setup():
        import jax, jax.numpy as jnp
        import numpy as np
        N_NODES = 6250
        N_FEAT = 96
        N_EDGES = 100000
        K_HOPS = 2
        key = jax.random.key(seed)
        k1, k2 = jax.random.split(key)
        x = jax.random.normal(k1, (N_NODES, N_FEAT), dtype=jnp.float32)
        edge_index = jax.random.randint(k2, (2, N_EDGES), 0, N_NODES, dtype=jnp.int64)
        return {'x': x, 'edge_index': edge_index}
    _L2_gnn_all = _L2_gnn_setup()
    _L2_gnn_in = {k: v for k, v in _L2_gnn_all.items() if k in ()}
    del _L2_gnn_all

    def _L3_gnn_setup():
        import jax, jax.numpy as jnp
        import numpy as np
        N_NODES = 6250
        N_EDGES = 100000
        IN_FEATS = 96
        OUT_FEATS = 96
        key = jax.random.key(seed)
        k1, k2, k3, k4, k5 = jax.random.split(key, 5)
        feat = jax.random.normal(k1, (N_NODES, IN_FEATS), dtype=jnp.float32)
        weight = jax.random.normal(k2, (IN_FEATS, OUT_FEATS), dtype=jnp.float32) * 0.05
        bias = jax.random.normal(k3, (OUT_FEATS,), dtype=jnp.float32) * 0.05
        src = jax.random.randint(k4, (N_EDGES,), 0, N_NODES, dtype=jnp.int64 if jax.config.jax_enable_x64 else jnp.int32)
        dst = jax.random.randint(k5, (N_EDGES,), 0, N_NODES, dtype=jnp.int64 if jax.config.jax_enable_x64 else jnp.int32)
        return {'feat': feat, 'weight': weight, 'bias': bias, 'src': src, 'dst': dst}
    _L3_gnn_all = _L3_gnn_setup()
    _L3_gnn_in = {k: v for k, v in _L3_gnn_all.items() if k in ('weight', 'bias')}
    del _L3_gnn_all
    return {'x': x, 'src': src, 'dst': dst, 'edge_attr_17': edge_attr_17, 'edge_attr_32': edge_attr_32, 'L0_gnn_W1_msg': _L0_gnn_in['W1_msg'], 'L0_gnn_W1_edge': _L0_gnn_in['W1_edge'], 'L0_gnn_W1_root': _L0_gnn_in['W1_root'], 'L0_gnn_b1': _L0_gnn_in['b1'], 'L0_gnn_W2_msg': _L0_gnn_in['W2_msg'], 'L0_gnn_W2_edge': _L0_gnn_in['W2_edge'], 'L0_gnn_W2_root': _L0_gnn_in['W2_root'], 'L0_gnn_b2': _L0_gnn_in['b2'], 'L1_gnn_W1': _L1_gnn_in['W1'], 'L1_gnn_b1': _L1_gnn_in['b1'], 'L1_gnn_W2': _L1_gnn_in['W2'], 'L1_gnn_b2': _L1_gnn_in['b2'], 'L1_gnn_Ws': _L1_gnn_in['Ws'], 'L1_gnn_bs': _L1_gnn_in['bs'], 'L1_gnn_Wn': _L1_gnn_in['Wn'], 'L1_gnn_bn': _L1_gnn_in['bn'], 'L3_gnn_weight': _L3_gnn_in['weight'], 'L3_gnn_bias': _L3_gnn_in['bias']}

def reference(x, src, dst, edge_attr_17, edge_attr_32, L0_gnn_W1_msg, L0_gnn_W1_edge, L0_gnn_W1_root, L0_gnn_b1, L0_gnn_W2_msg, L0_gnn_W2_edge, L0_gnn_W2_root, L0_gnn_b2, L1_gnn_W1, L1_gnn_b1, L1_gnn_W2, L1_gnn_b2, L1_gnn_Ws, L1_gnn_bs, L1_gnn_Wn, L1_gnn_bn, L3_gnn_weight, L3_gnn_bias):
    import jax
    import jax.numpy as jnp

    def _L0_gnn_ref(X, edge_index, edge_attr, W1_msg, W1_edge, W1_root, b1, W2_msg, W2_edge, W2_root, b2):
        import jax, jax.numpy as jnp
        import numpy as np
        N, E = (6250, 100000)
        DIN = DOUT = 96
        DE = 32

        def _egnn_conv(x, src, dst, edge_attr, W_msg, W_edge, W_root, b):
            msg = x[src] @ W_msg + edge_attr @ W_edge
            agg = jax.ops.segment_max(msg, dst, num_segments=x.shape[0])
            agg = jnp.where(jnp.isneginf(agg), 0.0, agg)
            return agg + x @ W_root + b
        src, dst = (edge_index[0], edge_index[1])
        c1 = jax.nn.leaky_relu(_egnn_conv(X, src, dst, edge_attr, W1_msg, W1_edge, W1_root, b1))
        c2 = jax.nn.leaky_relu(_egnn_conv(c1, src, dst, edge_attr, W2_msg, W2_edge, W2_root, b2))
        return c2

    def _L1_gnn_ref(x, edge_index, edge_attr, W1, b1, W2, b2, Ws, bs, Wn, bn):
        import jax, jax.numpy as jnp
        import numpy as np
        N = 6250
        E = 100000
        D = 96
        ED = 17
        src, dst = (edge_index[0], edge_index[1])
        h = jax.nn.relu(edge_attr @ W1.T + b1)
        w = h @ W2.T + b2
        msg = w * x[src]
        agg = jax.ops.segment_sum(msg, dst, num_segments=x.shape[0])
        return jax.nn.relu(x @ Ws.T + bs + agg @ Wn.T + bn)

    def _L2_gnn_ref(x, edge_index):
        import jax, jax.numpy as jnp
        import numpy as np
        N_NODES = 6250
        N_FEAT = 96
        N_EDGES = 100000
        K_HOPS = 2
        N = x.shape[0]
        loops = jnp.arange(N, dtype=edge_index.dtype)
        src = jnp.concatenate([edge_index[0], loops])
        dst = jnp.concatenate([edge_index[1], loops])
        ew = jnp.ones(src.shape[0], dtype=x.dtype)
        deg = jax.ops.segment_sum(ew, dst, num_segments=N)
        deg_inv_sqrt = jnp.where(deg > 0, jax.lax.rsqrt(deg), jnp.zeros_like(deg))
        norm = deg_inv_sqrt[src] * ew * deg_inv_sqrt[dst]

        def hop(h):
            return jax.ops.segment_sum(norm[:, None] * h[src], dst, num_segments=N)
        h = x
        for _ in range(K_HOPS):
            h = hop(h)
        return h

    def _L3_gnn_ref(feat, weight, bias, src, dst):
        import jax, jax.numpy as jnp
        import numpy as np
        N_NODES = 6250
        N_EDGES = 100000
        IN_FEATS = 96
        OUT_FEATS = 96
        N = feat.shape[0]
        ones = jnp.ones(src.shape, dtype=feat.dtype)
        out_deg = jnp.clip(jax.ops.segment_sum(ones, src, num_segments=N), 1.0)
        in_deg = jnp.clip(jax.ops.segment_sum(ones, dst, num_segments=N), 1.0)
        feat_n = feat * (out_deg ** (-0.5))[:, None]
        agg = jax.ops.segment_sum(feat_n[src], dst, num_segments=N)
        rst = agg @ weight
        rst = rst * (in_deg ** (-0.5))[:, None]
        return rst + bias
    edge_index = jnp.stack([src, dst])
    x = _layernorm(x + _L0_gnn_ref(x, edge_index, edge_attr_32, L0_gnn_W1_msg, L0_gnn_W1_edge, L0_gnn_W1_root, L0_gnn_b1, L0_gnn_W2_msg, L0_gnn_W2_edge, L0_gnn_W2_root, L0_gnn_b2), axis=-1)
    x = _layernorm(x + _L1_gnn_ref(x, edge_index, edge_attr_17, L1_gnn_W1, L1_gnn_b1, L1_gnn_W2, L1_gnn_b2, L1_gnn_Ws, L1_gnn_bs, L1_gnn_Wn, L1_gnn_bn), axis=-1)
    x = _layernorm(x + _L2_gnn_ref(x, edge_index), axis=-1)
    x = _layernorm(x + _L3_gnn_ref(x, L3_gnn_weight, L3_gnn_bias, src, dst), axis=-1)
    return x

_drawn_inputs = setup_inputs


def setup_inputs(seed=0):
    import zlib

    import numpy as np

    out = dict(_drawn_inputs(seed))
    spreads = {'L0_gnn_b1': (0.0, 0.1), 'L0_gnn_b2': (0.0, 0.339)}
    factors = {}
    for name, (base, spread) in spreads.items():
        noise = np.random.default_rng([zlib.crc32(name.encode()), seed]).standard_normal(out[name].shape)
        drawn = base * np.exp(spread * noise) if base else spread * noise
        out[name] = jnp.asarray(drawn.astype(out[name].dtype))
    for name, factor in factors.items():
        out[name] = (out[name] * factor).astype(out[name].dtype)
    return out
```

```python
from contextlib import ExitStack

import concourse.bass as bass
from concourse import mybir

F32 = mybir.dt.float32
BF16 = mybir.dt.bfloat16
I32 = mybir.dt.int32
ALU = mybir.AluOpType
ACT = mybir.ActivationFunctionType
AX = mybir.AxisListType

N, E, D = 6250, 106250, 96
DE32, DE17 = 32, 17
P = 128
QT = 4
Q = QT * P
CT = 4 * QT
CHUNK = CT * P
PAIRS = -(-E // (2 * CHUNK))
EP = PAIRS * 2 * CHUNK
TILES = EP // P
QUARTERS = 8 * PAIRS
GT = 5
GROUPS = 10
GPAIRS = GROUPS // 2
NT = GT * GROUPS
NP = NT * P
GN = GT * P
GF = GT * D
LAG = 5
BIG = 3.3895313892515355e38
EPS = 1e-5
SLOPE = 0.01

PASSES = 6
EDGE32, EDGE17, PLAIN = "edge32", "edge17", "plain"
KIND = [EDGE32, EDGE32, EDGE17, PLAIN, PLAIN, PLAIN]
IS_MAX = [True, True, False, False, False, False]
HISTOGRAM = {0: "dst", 3: "src"}


def gnn_kernel(nc, x_nodes, x_t, src_t, dst_t, dst_now, dst_before, ea17_t, ea32_t,
               w_l0_msg1, w_l0_root1, w_l0_edge1, w_l0_msg2, w_l0_root2, w_l0_edge2,
               w_edge_in, b_edge_in, w_edge_out, w_self, w_neigh, w_l3, out):
    tables = [nc.dram_tensor(f"table{p}", [NP, D], F32).ap() for p in range(PASSES)]
    rows = nc.dram_tensor("scanned_rows", [EP + 1, D], F32).ap()
    keep_sum_d = nc.dram_tensor("keep_sum_d", [1, EP], BF16).ap()
    keep_max_d = nc.dram_tensor("keep_max_d", [1, EP], BF16).ap()
    rows_v = rows[0:EP, :].rearrange("(c p j) f -> p c (j f)", p=P, j=CT)
    tables_v = [t.rearrange("(t p) f -> p t f", p=P) for t in tables]
    x_v = x_nodes.rearrange("(t p) f -> p t f", p=P)
    out_v = out.rearrange("(t p) f -> p t f", p=P)

    ctx = ExitStack()
    with ctx:
        def sb(name, shape, dt=F32):
            return ctx.enter_context(nc.sbuf_tensor(name, shape, dt))

        def sem(name):
            return ctx.enter_context(nc.semaphore(name))

        src_ix = sb("src_ix", [P, 2, CT], I32)
        gath = sb("gath", [P, 2, CT, D])
        ea = sb("ea", [DE32, 2, CHUNK])
        keep = sb("keep", [D, 2, CHUNK], BF16)
        msg = sb("msg", [P, 2, QT * D])
        hid = sb("hid", [D + 1, 2, Q])
        scan = sb("scan", [D, 2, CHUNK])
        back = sb("back", [P, 2, CT * D])
        hot_lo = sb("hot_lo", [P, 2, QT, P], BF16)
        hot_hi = sb("hot_hi", [P, 2, QT, NT], BF16)
        x_sb = sb("x_sb", [P, NT, D])
        r_sb = sb("r_sb", [P, NT, D])
        agg = sb("agg", [P, 2, GT, D])
        node = sb("node", [P, 2, GT, D])
        node_t = sb("node_t", [D + 1, 2, GN])
        y = sb("y", [P, 2, GT, D])
        v = sb("v", [P, 2, GT, D])
        sq = sb("sq", [P, GT, D])
        mean = sb("mean", [P, GT])
        var = sb("var", [P, 2, GT])
        dev = sb("dev", [P, 2, GT])
        end_ix = sb("end_ix", [P, 2, GT], I32)
        ends = sb("ends", [P, NT], I32)
        ids = sb("ids", [P, 2, TILES], I32)
        part = sb("part", [P, TILES], I32)
        lo = {k: sb(f"lo_{k}", [P, TILES], BF16) for k in ("dst", "src")}
        hi = {k: sb(f"hi_{k}", [P, TILES], BF16) for k in ("dst", "src")}
        flag = sb("flag", [P, TILES])
        keep_s = sb("keep_s", [P, TILES], BF16)
        keep_m = sb("keep_m", [P, TILES], BF16)
        deg = sb("deg", [P, NT])
        below = sb("below", [P, NT])
        tile_sum = sb("tile_sum", [P, NT])
        has = sb("has", [P, NT])
        norms = sb("norms", [P, 2, NT])
        roots = sb("roots", [P, 2, NT])
        dis, inn = norms[:, 0, :], norms[:, 1, :]
        dis2 = sb("dis2", [P, NT])
        outn = sb("outn", [P, NT])
        ident = sb("ident", [P, P])
        upper = sb("upper", [P, P])
        ones = sb("ones", [P, P])
        iota_i = sb("iota_i", [P, P], I32)
        iota_b = sb("iota_b", [P, P], BF16)
        zero_row = sb("zero_row", [1, D])
        W = {}
        loads = [("msg1", w_l0_msg1), ("root1", w_l0_root1), ("edge1", w_l0_edge1),
                 ("msg2", w_l0_msg2), ("root2", w_l0_root2), ("edge2", w_l0_edge2),
                 ("edge_in", w_edge_in), ("edge_in_b", b_edge_in), ("edge_out", w_edge_out),
                 ("self", w_self), ("neigh", w_neigh), ("l3", w_l3)]
        for name, ap in loads:
            W[name] = sb(f"w_{name}", list(ap.shape))

        banks = ctx.enter_context(nc.psum_tensor("banks", [P, 8, 512], F32))
        back_ps = [banks[:, b, 0:QT * D] for b in (0, 1)]
        w_ps = [banks[:, b, 0:QT * D] for b in (2, 3)]
        turn_ps = [banks[0:D, b, :] for b in (4, 5)]
        hid_ps = [banks[0:D, b, :] for b in (6, 7)]
        hist_ps = banks[:, 6, 0:NT]
        pre_ps = banks[:, 7, 0:2 * NT]
        node_turn_ps = banks[0:D, 2:4, :].rearrange("p b c -> p (b c)")[:, 0:GN]
        y_ps = [banks[:, b, 0:GF] for b in (4, 5)]
        r_ps = [banks[:, b, 0:GF] for b in (6, 7)]

        s_weights = sem("s_weights")
        s_ids = sem("s_ids")
        s_seq = sem("s_seq")
        s_const = sem("s_const")
        s_split = sem("s_split")
        s_keep_made = sem("s_keep_made")
        s_keep_out = sem("s_keep_out")
        s_x = sem("s_x")
        s_ix = [sem(f"s_ix{b}") for b in (0, 1)]
        s_ea = [sem(f"s_ea{b}") for b in (0, 1)]
        s_keep = [sem(f"s_keep{b}") for b in (0, 1)]
        s_gath = [sem(f"s_gath{k}") for k in range(8)]
        s_hid_ps = sem("s_hid_ps")
        s_hid = sem("s_hid")
        s_w = sem("s_w")
        s_msg = sem("s_msg")
        s_turn = sem("s_turn")
        s_scan = sem("s_scan")
        s_back = sem("s_back")
        s_evac = sem("s_evac")
        s_rows = [sem(f"s_rows{b}") for b in (0, 1)]
        s_passed = sem("s_passed")
        s_sp_passed = sem("s_sp_passed")
        s_hot = sem("s_hot")
        s_hist = sem("s_hist")
        s_deg = sem("s_deg")
        s_prefix = sem("s_prefix")
        s_ends = sem("s_ends")
        s_roots = sem("s_roots")
        NODE = range(PASSES + 1)
        s_nt_in = [sem(f"s_nt_in{b}") for b in (0, 1)]
        s_end_ix = [sem(f"s_end_ix_{n}") for n in NODE]
        s_agg = [[sem(f"s_agg{b}_{n}") for b in (0, 1)] for n in NODE]
        s_agg_used = [sem(f"s_agg_used_{n}") for n in NODE]
        s_node = [sem(f"s_node_{n}") for n in NODE]
        s_nturn = [sem(f"s_nturn_{n}") for n in NODE]
        s_nt = [sem(f"s_nt_{n}") for n in NODE]
        s_mm = [sem(f"s_mm_{n}") for n in NODE]
        s_copied = [sem(f"s_copied_{n}") for n in NODE]
        s_y = [sem(f"s_y_{n}") for n in NODE]
        s_var = [sem(f"s_var_{n}") for n in NODE]
        s_dev = [sem(f"s_dev_{n}") for n in NODE]
        s_table = [[sem(f"s_table{b}_{n}") for b in (0, 1)] for n in NODE]

        def over_pairs(eng, pair):
            pair(0, True, False)
            with eng.Fori(1, PAIRS - 1) as i:
                pair(i, False, False)
            pair(PAIRS - 1, False, True)

        def over_groups(eng, *stages):
            def step(i, b, known):
                for stage, lag in stages:
                    g = 2 * i + b - lag if known else None
                    if not known or 0 <= g < GROUPS:
                        stage(i + (b - lag) // 2, (b - lag) % 2, known and g < 2)
            for s in range(4):
                step(s // 2, s % 2, True)
            with eng.Fori(2, GPAIRS) as i:
                step(i, 0, False)
                step(i, 1, False)
            for s in range(GROUPS, GROUPS + max(lag for _, lag in stages)):
                step(s // 2, s % 2, True)

        def under(i, k, n):
            return type(i) is int and 8 * i + k < n

        def of_group(table, i, b):
            return table[:, bass.ds((2 * i + b) * GT, GT), :]

        def spread(table, i, b):
            return table[:, bass.ds((2 * i + b) * GT, GT)].unsqueeze(2).to_broadcast([P, GT, D])

        block = ctx.enter_context(nc.Block())

        @block.sync
        def _(sp):
            sp.dma_start(part[:, :], dst_now).then_inc(s_seq, 16)
            sp.dma_start(flag[:, :].bitcast(I32), dst_before).then_inc(s_seq, 16)
            for name, ap in loads:
                sp.dma_start(W[name][:, :], ap).then_inc(s_weights, 16)

            def load_x_t(i, b, first):
                if not first:
                    sp.wait_ge(s_mm[0], 2 * i + b - 1)
                sp.dma_start(node_t[0:D, b, :], x_t[:, bass.ds((2 * i + b) * GN, GN)]).then_inc(s_nt_in[b], 16)

            def store_y(n, table):
                def group(i, b, first):
                    sp.wait_ge(s_y[n], 2 * i + b + 1)
                    sp.dma_start(of_group(table, i, b), y[:, b, :, :]).then_inc(s_table[n][b], 16)
                return group

            def load_and_store(i, b, first):
                load_x_t(i, b, first)
                if first and b == 0:
                    sp.dma_start(ids[:, 0, :], dst_t).then_inc(s_ids, 16)
                    sp.dma_start(ids[:, 1, :], src_t).then_inc(s_ids, 16)
                    sp.dma_start(x_sb[:, :, :], x_v).then_inc(s_x, 16)
                    sp.wait_ge(s_const, 5)
                    sp.dma_start(rows[EP:EP + 1, :], zero_row[:, :]).then_inc(s_rows[1], 16)
                    sp.wait_ge(s_keep_made, 2)
                    sp.dma_start(keep_sum_d[0, :].rearrange("(p n) -> p n", p=P), keep_s[:, :]).then_inc(s_keep_out, 16)
                    sp.dma_start(keep_max_d[0, :].rearrange("(p n) -> p n", p=P), keep_m[:, :]).then_inc(s_keep_out, 16)
                store_y(0, tables_v[0])(i, b, first)

            over_groups(sp, (load_and_store, 0))
            sp.wait_ge(s_keep_out, 32)

            for p in range(PASSES):
                edge_src = {EDGE32: ea32_t, EDGE17: ea17_t}.get(KIND[p])
                edge_k = {EDGE32: DE32, EDGE17: DE17}.get(KIND[p])
                keep_d = keep_max_d if IS_MAX[p] else keep_sum_d

                def loads_of_pair(i, first, last):
                    for b in (0, 1):
                        q = 8 * i + 4 * b
                        if not first:
                            for k in range(4):
                                sp.wait_ge(s_gath[4 * b + k], 16 * QT * (PAIRS * p + i))
                        sp.dma_start(src_ix[:, b, :], src_t[:, bass.ds(CT * (2 * i + b), CT)]).then_inc(s_ix[b], 16)
                        at = bass.ds(CHUNK * (2 * i + b), CHUNK)
                        if edge_src is not None:
                            if not first:
                                if KIND[p] == EDGE17:
                                    sp.wait_ge(s_hid_ps, q - 4)
                                else:
                                    sp.wait_ge(s_w, QUARTERS * p + q - 4)
                            sp.dma_start(ea[0:edge_k, b, :], edge_src[:, at]).then_inc(s_ea[b], 16)
                        if not first:
                            sp.wait_ge(s_scan, QUARTERS * p + q - 4)
                            sp.sem_inc(s_sp_passed, 1)
                        sp.dma_start(keep[:, b, :], keep_d[0:1, at].to_broadcast([D, CHUNK])).then_inc(s_keep[b], 16)

                over_pairs(sp, loads_of_pair)

                n = p + 1
                if p == 0:
                    over_groups(sp, (store_y(n, tables_v[1]), 0))
                elif p == 1:
                    def store_node(i, b, first):
                        sp.wait_ge(s_node[n], 2 * i + b + 1)
                        sp.dma_start(of_group(tables_v[2], i, b), node[:, b, :, :]).then_inc(s_table[n][b], 16)
                    over_groups(sp, (store_node, 0))
                elif p < 5:
                    def store_r(i, b, first):
                        sp.wait_ge(s_y[n], 2 * i + b + 1)
                        sp.dma_start(of_group(tables_v[p + 1], i, b), of_group(r_sb, i, b)).then_inc(s_table[n][b], 16)
                    over_groups(sp, (store_r, 0))
                else:
                    over_groups(sp, (store_y(n, out_v), 0))
            for b in (0, 1):
                sp.wait_ge(s_table[PASSES][b], 16 * GPAIRS)

        @block.gpsimd
        def _(pool):
            pool.memset(ident[:, :], 1.0)
            pool.memset(upper[:, :], 1.0)
            pool.memset(ones[:, :], 1.0)
            pool.memset(zero_row[:, :], 0.0)
            pool.iota(iota_i[:, :], [[1, P]], base=0, channel_multiplier=0).then_inc(s_const, 1)
            pool.drain()
            pool.tensor_copy(iota_b[:, :], iota_i[:, :]).then_inc(s_const, 1)
            pool.affine_select(out=ident[:, :], in_=ident[:, :], compare_op=ALU.is_equal, fill=0.0, base=0,
                               pattern=[[-1, P]], channel_multiplier=1).then_inc(s_const, 1)
            pool.affine_select(out=upper[:, :], in_=upper[:, :], compare_op=ALU.is_ge, fill=0.0, base=0,
                               pattern=[[1, P]], channel_multiplier=-1).then_inc(s_const, 1)

            for p in range(PASSES):
                for b in (0, 1):
                    pool.wait_ge(s_table[p][b], 16 * GPAIRS)

                def gather_pair(i, first, last):
                    for b in (0, 1):
                        pool.wait_ge(s_ix[b], 16 * (PAIRS * p + i + 1))
                        for k in range(4):
                            if not first:
                                q = QUARTERS * p + 8 * i + 4 * b + k - 7
                                pool.wait_ge(s_turn if KIND[p] == PLAIN else s_msg, q)
                            pool.sem_inc(s_passed, 1)
                            for t in range(QT * k, QT * k + QT):
                                pool.indirect_dma_start(
                                    gath[:, b, t, :], None, tables[p][:, :],
                                    bass.IndirectOffsetOnAxis(ap=src_ix[:, b, t:t + 1], axis=0),
                                ).then_inc(s_gath[4 * b + k], 16)

                over_pairs(pool, gather_pair)

                n = p + 1
                for b in (0, 1):
                    pool.wait_ge(s_rows[b], 16 * (PAIRS * (p + 1) + b))
                if p == 0:
                    pool.wait_ge(s_ends, 1)

                def gather_ends(i, b, first):
                    if not first:
                        pool.wait_ge({2: s_nturn, 5: s_node}.get(p, s_agg_used)[n], 2 * i + b - 1)
                    pool.tensor_copy(end_ix[:, b, :], ends[:, bass.ds((2 * i + b) * GT, GT)]).then_inc(s_end_ix[n], 1)
                    pool.wait_ge(s_end_ix[n], 2 * i + b + 1)
                    pool.sem_inc(s_passed, 1)
                    for t in range(GT):
                        pool.indirect_dma_start(
                            agg[:, b, t, :], None, rows[:, :],
                            bass.IndirectOffsetOnAxis(ap=end_ix[:, b, t:t + 1], axis=0),
                        ).then_inc(s_agg[n][b], 16)

                over_groups(pool, (gather_ends, 0))

        @block.tensor
        def _(pe):
            pe.wait_ge(s_const, 5)
            pe.wait_ge(s_weights, 16 * len(loads))

            def products(n, b, weights):
                for to, w in zip((y_ps[b], r_ps[b]), weights):
                    if w is None:
                        continue
                    k = W[w].shape[0]
                    for t in range(GT):
                        m = pe.matmul(to[:, t * D:(t + 1) * D], node_t[0:k, b, t * P:(t + 1) * P], W[w][:, :],
                                      start=True, stop=True)
                m.then_inc(s_mm[n], 1)

            def project_x(i, b, first):
                pe.wait_ge(s_nt_in[b], 16 * (i + 1))
                if not first:
                    pe.wait_ge(s_copied[0], 2 * i + b - 1)
                products(0, b, ("msg1", "root1"))

            over_groups(pe, (project_x, 0))

            for p in range(PASSES):
                base = QUARTERS * p
                if p < 3:
                    pe.wait_ge(s_copied[p], GROUPS)

                def hidden(i, k):
                    b, at = k // 4, k % 4 * Q
                    if at == 0:
                        pe.wait_ge(s_ea[b], 16 * (PAIRS * p + i + 1))
                    if not under(i, k, 2):
                        pe.wait_ge(s_hid, 8 * i + k - 1)
                    pe.matmul(hid_ps[k % 2], W["edge_in"][:, :], ea[0:DE17, b, at:at + Q],
                              start=True, stop=True).then_inc(s_hid_ps, 1)

                def edge_rows(i, k):
                    b, at = k // 4, k % 4 * Q
                    if not under(i, k, 2):
                        pe.wait_ge(s_msg, base + 8 * i + k - 1)
                    if KIND[p] == EDGE17:
                        pe.wait_ge(s_hid, 8 * i + k + 1)
                    elif at == 0:
                        pe.wait_ge(s_ea[b], 16 * (PAIRS * p + i + 1))
                    for t in range(QT):
                        if KIND[p] == EDGE17:
                            lhs, w = hid[:, k % 2, t * P:(t + 1) * P], W["edge_out"]
                        else:
                            lhs, w = ea[0:DE32, b, at + t * P:at + (t + 1) * P], W["edge1" if p == 0 else "edge2"]
                        m = pe.matmul(w_ps[k % 2][:, t * D:(t + 1) * D], lhs, w[:, :], start=True, stop=True)
                    m.then_inc(s_w, 1)

                def turn(i, k):
                    if KIND[p] == PLAIN:
                        pe.wait_ge(s_gath[k], 16 * QT * (PAIRS * p + i + 1))
                    else:
                        pe.wait_ge(s_msg, base + 8 * i + k + 1)
                    if not under(i, k, 2):
                        pe.wait_ge(s_scan, base + 8 * i + k - 1)
                    for t in range(QT):
                        if KIND[p] == PLAIN:
                            rows_in = gath[:, k // 4, QT * (k % 4) + t, :]
                        else:
                            rows_in = msg[:, k % 2, t * D:(t + 1) * D]
                        m = pe.transpose(turn_ps[k % 2][:, t * P:(t + 1) * P], rows_in, ident[:, :])
                    m.then_inc(s_turn, 1)

                def turn_back(i, k, first):
                    if first and k < LAG:
                        return
                    g8 = (k - LAG) % 8
                    b, g = g8 // 4, g8 % 4
                    if g == 0:
                        pe.wait_ge(s_scan, base + 8 * i + k - LAG + 4)
                    if not (first and k < LAG + 2):
                        pe.wait_ge(s_evac, base + 8 * i + k - LAG - 1)
                    for t in range(QT):
                        m = pe.transpose(back_ps[g8 % 2][:, t * D:(t + 1) * D],
                                         scan[:, b, QT * g + t:CHUNK:CT], ident[0:D, 0:D])
                    m.then_inc(s_back, 1)

                hist_base = QUARTERS * (p // 3)

                def count(i, k, first, last):
                    if p not in HISTOGRAM or (first and k < 2):
                        return
                    h = k % 2
                    pe.wait_ge(s_hot, hist_base + 8 * i + k - 1)
                    for t in range(QT):
                        m = pe.matmul(hist_ps, hot_lo[:, h, t, :], hot_hi[:, h, t, :],
                                      start=first and k == 2 and t == 0, stop=last and k == 1 and t == QT - 1,
                                      skip_group_check=True)
                    m.then_inc(s_hist, 1)

                if KIND[p] == EDGE17:
                    hidden(0, 0)
                    hidden(0, 1)
                if KIND[p] != PLAIN:
                    edge_rows(0, 0)

                def pair(i, first, last):
                    for k in range(8):
                        if KIND[p] == EDGE17 and not (last and k > 5):
                            hidden(i + (k + 2) // 8, (k + 2) % 8)
                        if KIND[p] != PLAIN and not (last and k == 7):
                            edge_rows(i + (k + 1) // 8, (k + 1) % 8)
                        turn_back(i, k, first)
                        count(i, k, first, False)
                        turn(i, k)

                over_pairs(pe, pair)
                for k in range(LAG):
                    if k < 2:
                        count(PAIRS, k, False, True)
                    turn_back(PAIRS, k, False)

                n = p + 1
                if p == 0:
                    pe.wait_ge(s_deg, 1)
                    pe.matmul(pre_ps[:, 0:NT], upper[:, :], deg[:, :], start=True, stop=True)
                    pe.matmul(pre_ps[:, NT:2 * NT], ones[:, :], deg[:, :], start=True, stop=True).then_inc(s_prefix, 1)
                    pe.wait_ge(s_ends, 1)

                def turn_nodes(i, b, first):
                    if p == 2:
                        pe.wait_ge(s_agg[n][b], 16 * GT * (i + 1))
                    else:
                        pe.wait_ge(s_node[n], 2 * i + b + 1)
                    if not (first and b == 0):
                        pe.wait_ge(s_nt[n], 2 * i + b)
                    for t in range(GT):
                        m = pe.transpose(node_turn_ps[:, t * P:(t + 1) * P],
                                         agg[:, b, t, :] if p == 2 else node[:, b, t, :], ident[:, :])
                    m.then_inc(s_nturn[n], 1)

                weights = {0: ("msg2", "root2"), 1: (None, "self"), 2: ("neigh", None), 5: ("l3", None)}.get(p)

                def multiply(i, b, first):
                    pe.wait_ge(s_nt[n], 2 * i + b + 1)
                    if not first:
                        pe.wait_ge(s_copied[n], 2 * i + b - 1)
                    products(n, b, weights)

                if weights:
                    over_groups(pe, (turn_nodes, 0), (multiply, 1))

        @block.scalar
        def _(act):
            def leave_x(i, b, first):
                if not first:
                    act.wait_ge(s_table[0][b], 16 * i)
                act.wait_ge(s_mm[0], 2 * i + b + 1)
                act.activation(y[:, b, :, :], y_ps[b].rearrange("p (t f) -> p t f", f=D), ACT.Copy).then_inc(s_y[0], 1)
                act.activation(of_group(r_sb, i, b), r_ps[b].rearrange("p (t f) -> p t f", f=D), ACT.Copy)\
                   .then_inc(s_copied[0], 1)

            over_groups(act, (leave_x, 0))

            for p in range(PASSES):
                base = QUARTERS * p

                def hidden_relu(i, k):
                    act.wait_ge(s_hid_ps, 8 * i + k + 1)
                    if not under(i, k, 2):
                        act.wait_ge(s_w, base + 8 * i + k - 1)
                    act.activation(hid[0:D, k % 2, :], hid_ps[k % 2], ACT.Relu, bias=W["edge_in_b"][:, 0:1])\
                       .then_inc(s_hid, 1)

                def evacuate(i, k, first):
                    if first and k < LAG:
                        return
                    g8 = (k - LAG) % 8
                    b, g = g8 // 4, g8 % 4
                    turn_i = i if k >= LAG else i - 1
                    if g == 0 and not (p == 0 and first):
                        act.wait_ge(s_rows[b], 16 * (PAIRS * p + turn_i + b))
                    act.wait_ge(s_back, base + 8 * i + k - LAG + 1)
                    act.activation(back[:, b, g * QT * D:(g + 1) * QT * D], back_ps[g8 % 2], ACT.Copy).then_inc(s_evac, 1)
                    if g == 3:
                        act.wait_ge(s_evac, base + 8 * i + k - LAG + 1)
                        act.dma_start(rows_v[:, bass.ds(2 * turn_i + b, 1), :].rearrange("p c x -> p (c x)"),
                                      back[:, b, :]).then_inc(s_rows[b], 16)

                if KIND[p] == EDGE17:
                    hidden_relu(0, 0)
                    hidden_relu(0, 1)

                def pair(i, first, last):
                    for k in range(8):
                        if KIND[p] == EDGE17 and not (last and k > 5):
                            hidden_relu(i + (k + 2) // 8, (k + 2) % 8)
                        evacuate(i, k, first)

                over_pairs(act, pair)
                for k in range(LAG):
                    evacuate(PAIRS, k, False)

                n = p + 1
                if p == 0:
                    act.wait_ge(s_deg, 2)
                    act.activation(roots[:, :, :], norms[:, :, :], ACT.Sqrt).then_inc(s_roots, 1)
                if p == 3:
                    act.wait_ge(s_deg, 3)
                    act.activation(roots[:, 0, :], outn[:, :], ACT.Sqrt).then_inc(s_roots, 1)

                def take_turned(i, b, first):
                    act.wait_ge(s_nturn[n], 2 * i + b + 1)
                    if not first:
                        act.wait_ge(s_mm[n], 2 * i + b - 1)
                    act.activation(node_t[0:D, b, :], node_turn_ps, ACT.Copy).then_inc(s_nt[n], 1)

                def leave(i, b, first):
                    if p == 1:
                        act.activation(of_group(x_sb, i, b), node[:, b, :, :], ACT.Copy)
                    act.wait_ge(s_mm[n], 2 * i + b + 1)
                    if p == 0:
                        if not first:
                            act.wait_ge(s_table[n][b], 16 * i)
                        act.activation(y[:, b, :, :], y_ps[b].rearrange("p (t f) -> p t f", f=D), ACT.Copy)\
                           .then_inc(s_y[n], 1)
                    act.activation(of_group(r_sb, i, b), r_ps[b].rearrange("p (t f) -> p t f", f=D), ACT.Copy)\
                       .then_inc(s_copied[n], 1)

                def deviation(i, b, first):
                    act.wait_ge(s_var[n], 2 * i + b + 1)
                    act.activation(dev[:, b, :], var[:, b, :], ACT.Sqrt).then_inc(s_dev[n], 1)

                stages = {0: [(take_turned, 0), (leave, 1)],
                          1: [(deviation, 0), (take_turned, 1), (leave, 2)],
                          2: [(take_turned, 0), (deviation, 1)],
                          4: [(deviation, 0)],
                          5: [(take_turned, 0), (deviation, 1)]}.get(p)
                if stages:
                    over_groups(act, *stages)

        @block.vector
        def _(ve):
            ve.memset(hid[D:D + 1, :, :], 1.0)
            ve.memset(node_t[D:D + 1, :, :], 1.0).then_inc(s_const, 1)
            ve.wait_ge(s_seq, 32)
            ve.tensor_tensor(flag[:, :], part[:, :], flag[:, :].bitcast(I32), ALU.is_equal)
            ve.drain()
            ve.tensor_copy(keep_s[:, :], flag[:, :]).then_inc(s_keep_made, 1)
            ve.tensor_scalar(flag[:, :], flag[:, :], 2.0, -1.0, ALU.mult, ALU.add)
            ve.drain()
            ve.tensor_scalar(keep_m[:, :], flag[:, :], BIG, None, ALU.mult).then_inc(s_keep_made, 1)
            ve.wait_ge(s_ids, 32)
            for n, k in enumerate(("dst", "src")):
                ve.drain()
                ve.tensor_scalar(part[:, :], ids[:, n, :], 7, None, ALU.arith_shift_right)
                ve.tensor_scalar(ids[:, n, :], ids[:, n, :], P - 1, None, ALU.bitwise_and)
                ve.drain()
                ve.tensor_copy(hi[k][:, :], part[:, :])
                ve.tensor_copy(lo[k][:, :], ids[:, n, :])
            ve.wait_ge(s_const, 5)
            ve.wait_ge(s_x, 16)
            ve.drain()

            for p in range(PASSES):
                base = QUARTERS * p
                keep_op, take_op = (ALU.min, ALU.max) if IS_MAX[p] else (ALU.mult, ALU.add)

                def message(i, k):
                    ve.wait_ge(s_w, base + 8 * i + k + 1)
                    ve.wait_ge(s_gath[k], 16 * QT * (PAIRS * p + i + 1))
                    if not under(i, k, 2):
                        ve.wait_ge(s_turn, base + 8 * i + k - 1)
                    ve.tensor_tensor(msg[:, k % 2, :], w_ps[k % 2],
                                     gath[:, k // 4, QT * (k % 4):QT * (k % 4) + QT, :].rearrange("p t f -> p (t f)"),
                                     ALU.add if KIND[p] == EDGE32 else ALU.mult).then_inc(s_msg, 1)

                def scan_quarter(i, k, first):
                    b, at = k // 4, k % 4 * Q
                    if at == 0:
                        ve.wait_ge(s_keep[b], 16 * (PAIRS * p + i + 1))
                        if not first:
                            ve.wait_ge(s_back, base + 8 * i + k - 4)
                    if first and k == 0:
                        start = 0.0
                    else:
                        ve.wait_ge(s_scan, base + 8 * i + k)
                        start = scan[:, b, at - 1:at] if at else scan[:, 1 - b, CHUNK - 1:CHUNK]
                    ve.wait_ge(s_turn, base + 8 * i + k + 1)
                    ve.tensor_tensor_scan(scan[:, b, at:at + Q], keep[:, b, at:at + Q], turn_ps[k % 2],
                                          start, keep_op, take_op).then_inc(s_scan, 1)

                hist_base = QUARTERS * (p // 3)

                def one_hots(i, k, first):
                    if p not in HISTOGRAM:
                        return
                    side = HISTOGRAM[p]
                    h = k % 2
                    if not (first and k < 2):
                        ve.wait_ge(s_hist, hist_base + 8 * i + k - 1)
                    at = bass.ds((8 * i + k) * QT, QT)
                    ve.tensor_tensor(hot_lo[:, h, :, :], lo[side][:, at].unsqueeze(2).to_broadcast([P, QT, P]),
                                     iota_b[:, :].unsqueeze(1).to_broadcast([P, QT, P]), ALU.is_equal)
                    ve.tensor_tensor(hot_hi[:, h, :, :], hi[side][:, at].unsqueeze(2).to_broadcast([P, QT, NT]),
                                     iota_b[:, 0:NT].unsqueeze(1).to_broadcast([P, QT, NT]), ALU.is_equal)\
                      .then_inc(s_hot, 1)

                if KIND[p] != PLAIN:
                    message(0, 0)

                def pair(i, first, last):
                    for k in range(8):
                        if KIND[p] != PLAIN and not (last and k == 7):
                            message(i + (k + 1) // 8, (k + 1) % 8)
                        scan_quarter(i, k, first)
                        one_hots(i, k, first)

                over_pairs(ve, pair)

                if p == 0:
                    ve.wait_ge(s_hist, QUARTERS)
                    ve.tensor_copy(deg[:, :], hist_ps).then_inc(s_deg, 1)
                    ve.drain()
                    ve.tensor_scalar(norms[:, 0, :], deg[:, :], 1.0, None, ALU.add)
                    ve.tensor_scalar(norms[:, 1, :], deg[:, :], 1.0, None, ALU.max).then_inc(s_deg, 1)
                    ve.tensor_scalar(has[:, :], deg[:, :], 0.5, None, ALU.is_gt)
                    ve.wait_ge(s_prefix, 1)
                    ve.tensor_copy(tile_sum[:, :], pre_ps[:, NT:2 * NT])
                    ve.drain()
                    ve.tensor_tensor_scan(below[:, :], ones[:, 0:NT], tile_sum[:, :], 0.0, ALU.mult, ALU.add)
                    ve.drain()
                    ve.tensor_tensor(below[:, :], below[:, :], tile_sum[:, :], ALU.subtract)
                    ve.drain()
                    ve.tensor_tensor(below[:, :], below[:, :], pre_ps[:, 0:NT], ALU.add)
                    ve.drain()
                    ve.scalar_tensor_tensor(below[:, :], below[:, :], -1.0 - EP, has[:, :], ALU.add, ALU.mult)
                    ve.drain()
                    ve.tensor_scalar(ends[:, :], below[:, :], float(EP), None, ALU.add).then_inc(s_ends, 1)
                    ve.wait_ge(s_roots, 1)
                    ve.reciprocal(norms[:, :, :], roots[:, :, :])
                    ve.drain()
                    ve.tensor_tensor(dis2[:, :], dis, dis, ALU.mult)
                elif p == 3:
                    ve.wait_ge(s_hist, 2 * QUARTERS)
                    ve.tensor_scalar(outn[:, :], hist_ps, 1.0, None, ALU.max).then_inc(s_deg, 1)
                    ve.wait_ge(s_roots, 2)
                    ve.reciprocal(outn[:, :], roots[:, 0, :])
                    ve.drain()

                n = p + 1
                if p < 3:
                    ve.wait_ge(s_copied[p], GROUPS)

                def statistics(b):
                    vb = v[:, b, :, :]
                    ve.drain()
                    ve.tensor_reduce(mean[:, :], vb, AX.X, ALU.add)
                    ve.drain()
                    ve.tensor_scalar(mean[:, :], mean[:, :], 1.0 / D, None, ALU.mult)
                    ve.drain()
                    ve.tensor_tensor(vb, vb, mean[:, :].unsqueeze(2).to_broadcast([P, GT, D]), ALU.subtract)
                    ve.drain()
                    ve.tensor_tensor(sq[:, :, :], vb, vb, ALU.mult)
                    ve.drain()
                    ve.tensor_reduce(var[:, b, :], sq[:, :, :], AX.X, ALU.add)
                    ve.drain()
                    ve.tensor_scalar(var[:, b, :], var[:, b, :], 1.0 / D, EPS, ALU.mult, ALU.add)\
                      .then_inc(s_var[n], 1)

                def add_and_rectify(i, b, first):
                    ve.drain()
                    ve.wait_ge(s_agg[n][b], 16 * GT * (i + 1))
                    ve.tensor_tensor(v[:, b, :, :], agg[:, b, :, :], of_group(r_sb, i, b), ALU.add)\
                      .then_inc(s_agg_used[n], 1)
                    ve.drain()
                    if p == 0:
                        if not first:
                            ve.wait_ge(s_nturn[n], 2 * i + b - 1)
                        ve.scalar_tensor_tensor(node[:, b, :, :], v[:, b, :, :], SLOPE, v[:, b, :, :],
                                                ALU.mult, ALU.max).then_inc(s_node[n], 1)
                    else:
                        ve.scalar_tensor_tensor(sq[:, :, :], v[:, b, :, :], SLOPE, v[:, b, :, :], ALU.mult, ALU.max)
                        ve.drain()
                        ve.tensor_tensor(v[:, b, :, :], sq[:, :, :], of_group(x_sb, i, b), ALU.add)
                        statistics(b)

                def dense_sum(i, b, first):
                    products_in = y_ps[b].rearrange("p (t f) -> p t f", f=D)
                    ve.drain()
                    ve.wait_ge(s_mm[n], 2 * i + b + 1)
                    if p == 2:
                        ve.tensor_tensor(v[:, b, :, :], products_in, of_group(r_sb, i, b), ALU.add)\
                          .then_inc(s_copied[n], 1)
                        ve.drain()
                        ve.scalar_tensor_tensor(v[:, b, :, :], v[:, b, :, :], 0.0, of_group(x_sb, i, b), ALU.max, ALU.add)
                    else:
                        ve.tensor_tensor(v[:, b, :, :], products_in, of_group(x_sb, i, b), ALU.add)\
                          .then_inc(s_copied[n], 1)
                    statistics(b)

                def hop(i, b, first):
                    ve.drain()
                    ve.wait_ge(s_agg[n][b], 16 * GT * (i + 1))
                    ve.tensor_tensor(v[:, b, :, :], agg[:, b, :, :], of_group(r_sb, i, b), ALU.add)\
                      .then_inc(s_agg_used[n], 1)
                    ve.drain()
                    if p == 3:
                        ve.tensor_tensor(of_group(r_sb, i, b), v[:, b, :, :], spread(dis2, i, b), ALU.mult)\
                          .then_inc(s_y[n], 1)
                    else:
                        ve.tensor_tensor(v[:, b, :, :], v[:, b, :, :], spread(dis, i, b), ALU.mult)
                        ve.drain()
                        ve.tensor_tensor(v[:, b, :, :], v[:, b, :, :], of_group(x_sb, i, b), ALU.add)
                        statistics(b)

                def scale_in(i, b, first):
                    ve.wait_ge(s_agg[n][b], 16 * GT * (i + 1))
                    if not first:
                        ve.wait_ge(s_nturn[n], 2 * i + b - 1)
                    ve.tensor_tensor(node[:, b, :, :], agg[:, b, :, :], spread(inn, i, b), ALU.mult)\
                      .then_inc(s_node[n], 1)

                def normalise(i, b, first):
                    ve.drain()
                    ve.wait_ge(s_dev[n], 2 * i + b + 1)
                    ve.reciprocal(mean[:, :], dev[:, b, :])
                    ve.drain()
                    over = mean[:, :].unsqueeze(2).to_broadcast([P, GT, D])
                    if p == 1:
                        if not first:
                            ve.wait_ge(s_nturn[n], 2 * i + b - 1)
                            ve.wait_ge(s_copied[n], 2 * i + b - 1)
                            ve.wait_ge(s_table[n][b], 16 * i)
                        ve.tensor_tensor(node[:, b, :, :], v[:, b, :, :], over, ALU.mult).then_inc(s_node[n], 1)
                    elif p == 5:
                        if not first:
                            ve.wait_ge(s_table[n][b], 16 * i)
                        ve.tensor_tensor(y[:, b, :, :], v[:, b, :, :], over, ALU.mult).then_inc(s_y[n], 1)
                    else:
                        ve.tensor_tensor(of_group(x_sb, i, b), v[:, b, :, :], over, ALU.mult)
                        ve.drain()
                        ve.tensor_tensor(of_group(r_sb, i, b), of_group(x_sb, i, b),
                                         spread(dis if p == 2 else outn, i, b), ALU.mult).then_inc(s_y[n], 1)

                over_groups(ve, *{0: [(add_and_rectify, 0)],
                                  1: [(add_and_rectify, 0), (normalise, 1)],
                                  2: [(dense_sum, 0), (normalise, 1)],
                                  3: [(hop, 0)],
                                  4: [(hop, 0), (normalise, 1)],
                                  5: [(scale_in, 0), (dense_sum, 1), (normalise, 2)]}[p])


def kernel(x, src, dst, edge_attr_17, edge_attr_32, L0_gnn_W1_msg, L0_gnn_W1_edge, L0_gnn_W1_root, L0_gnn_b1,
           L0_gnn_W2_msg, L0_gnn_W2_edge, L0_gnn_W2_root, L0_gnn_b2, L1_gnn_W1, L1_gnn_b1, L1_gnn_W2, L1_gnn_b2,
           L1_gnn_Ws, L1_gnn_bs, L1_gnn_Wn, L1_gnn_bn, L3_gnn_weight, L3_gnn_bias):
    import numpy as np
    import concourse.bacc as bacc
    from concourse.bass_utils import run_bass_kernel_spmd

    def padded(a, size, fill=0):
        a = np.asarray(a)
        return np.concatenate([a, np.full((size - a.shape[0],) + a.shape[1:], fill, a.dtype)])

    src, dst = padded(src, EP, NP - 1), padded(dst, EP, NP - 1)
    x = padded(x, NP)
    before = np.concatenate([np.full((1,), -1, dst.dtype), dst[:-1]])
    inputs = {
        "x_nodes": x, "x_t": x.T,
        "src_t": src.reshape(TILES, P).T, "dst_t": dst.reshape(TILES, P).T,
        "dst_now": dst.reshape(P, TILES), "dst_before": before.reshape(P, TILES),
        "ea17_t": padded(edge_attr_17, EP).T, "ea32_t": padded(edge_attr_32, EP).T,
        "w_l0_msg1": L0_gnn_W1_msg, "w_l0_root1": np.vstack([L0_gnn_W1_root, L0_gnn_b1]), "w_l0_edge1": L0_gnn_W1_edge,
        "w_l0_msg2": L0_gnn_W2_msg, "w_l0_root2": np.vstack([L0_gnn_W2_root, L0_gnn_b2]), "w_l0_edge2": L0_gnn_W2_edge,
        "w_edge_in": np.asarray(L1_gnn_W1).T, "b_edge_in": np.asarray(L1_gnn_b1)[:, None],
        "w_edge_out": np.vstack([np.asarray(L1_gnn_W2).T, L1_gnn_b2]),
        "w_self": np.vstack([np.asarray(L1_gnn_Ws).T, L1_gnn_bs]),
        "w_neigh": np.vstack([np.asarray(L1_gnn_Wn).T, L1_gnn_bn]),
        "w_l3": np.vstack([L3_gnn_weight, L3_gnn_bias]),
    }
    nc = bacc.Bacc("TRN2", target_bir_lowering=False, num_devices=1)
    arrays, args = {}, {}
    for name, a in inputs.items():
        a = np.ascontiguousarray(a)
        arrays[f"in_{name}"] = a
        args[name] = nc.dram_tensor(f"in_{name}", a.shape, mybir.dt.from_np(a.dtype), kind="ExternalInput").ap()
    args["out"] = nc.dram_tensor("out_x", (NP, D), F32, kind="ExternalOutput").ap()
    gnn_kernel(nc, **args)
    result = run_bass_kernel_spmd(nc, [arrays], core_ids=[0])
    return result.results[0]["out_x"][:N]
```

```python
from contextlib import ExitStack

import concourse.bass as bass
from concourse import mybir

F32 = mybir.dt.float32
BF16 = mybir.dt.bfloat16
I32 = mybir.dt.int32
ALU = mybir.AluOpType
ACT = mybir.ActivationFunctionType
AX = mybir.AxisListType

N, E, D = 6250, 106250, 96
DE32 = 32
COPIES = (0, 64, 96)
PART_AT = (0, 64, 96)
P = 128
QT = 4
Q = QT * P
CT = 4 * QT
CHUNK = CT * P
PAIRS = -(-E // (2 * CHUNK))
EP = PAIRS * 2 * CHUNK
TILES = EP // P
QUARTERS = 8 * PAIRS
STORES = (PAIRS, PAIRS + 3)
GT = 5
GROUPS = 10
GPAIRS = GROUPS // 2
NT = GT * GROUPS
NP = NT * P
GN = GT * P
GF = GT * D
SPLIT_AT = {2: (1, 0, 0), 3: (1, 0, 1), 4: (1, 0, 2), 6: (1, 1, 0), 7: (1, 1, 1), 0: (0, 1, 2)}
LAG = 2
ROW = 2 * DE32 + 2
SRC_AT, DST_AT = 2 * DE32, 2 * DE32 + 1
BIG = 3.3895313892515355e38
EPS = 1e-5
SLOPE = 0.01

PASSES = 6
EDGE32, EDGE17, PLAIN = "edge32", "edge17", "plain"
KIND = [EDGE32, EDGE32, EDGE17, PLAIN, PLAIN, PLAIN]
IS_MAX = [True, True, False, False, False, False]
NORMED = (1, 2, 4, 5)
HISTOGRAM = {0: "dst", 3: "src"}


def gnn_kernel(nc, x_nodes, x_t, src_t, dst_t, dst_now, dst_before, ea17_t, ea32_t, ea17_rows, ea32_rows,
               w_l0_msg1, w_l0_root1, w_l0_edge1, w_l0_msg2, w_l0_root2, w_l0_edge2,
               w_edge_in, b_edge_in, w_edge_out, w_self, w_neigh, w_l3, out):
    tables = [nc.dram_tensor(f"table{p}", [NP, D], F32).ap() for p in range(PASSES)]
    rows = nc.dram_tensor("scanned_rows", [EP + 1, D], F32).ap()
    keep_sum_d = nc.dram_tensor("keep_sum_d", [1, EP], BF16).ap()
    keep_max_d = nc.dram_tensor("keep_max_d", [1, EP], BF16).ap()
    ordered = nc.dram_tensor("ordered", [EP, ROW], F32).ap()
    ordered_ea = {EDGE32: nc.dram_tensor("ordered_ea32_t", [DE32, EP], F32).ap(),
                  EDGE17: nc.dram_tensor("ordered_ea17_t", [DE32, EP], F32).ap()}
    ordered_src = nc.dram_tensor("ordered_src_t", [P, TILES], I32).ap()
    ordered_dst = nc.dram_tensor("ordered_dst", [1 + EP], I32).ap()
    dst_seq = dst_now.rearrange("p n -> (p n)").unsqueeze(0)
    rows_v = rows[0:EP, :].rearrange("(q p j) f -> p q (j f)", p=P, j=QT)
    tables_v = [t.rearrange("(t p) f -> p t f", p=P) for t in tables]
    x_v = x_nodes.rearrange("(t p) f -> p t f", p=P)
    out_v = out.rearrange("(t p) f -> p t f", p=P)

    bn_dim = nc.vector.BN_STATS_DIM
    ctx = ExitStack()
    with ctx:
        def sb(name, shape, dt=F32):
            return ctx.enter_context(nc.sbuf_tensor(name, shape, dt))

        def sem(name):
            return ctx.enter_context(nc.semaphore(name))

        src_ix = sb("src_ix", [P, 2, CT], I32)
        gath = sb("gath", [P, 2, CT, D])
        ea = sb("ea", [P, 2, CHUNK])
        parts = sb("parts", [P, 2, CHUNK], BF16)
        w_in = sb("w_in", [P, D])
        w_parts = [sb(f"w_parts{n}", [P, D], BF16) for n in range(3)]
        keep = sb("keep", [D, 2, CHUNK], BF16)
        msg = sb("msg", [P, 2, QT * D])
        hid = sb("hid", [D + 1, 2, Q])
        scan = sb("scan", [D + 1, 2, CHUNK])
        back = sb("back", [P, 2, CT * D])
        hot_lo = sb("hot_lo", [P, 2, QT, P], BF16)
        hot_hi = sb("hot_hi", [P, 2, QT, NT], BF16)
        x_sb = sb("x_sb", [P, NT, D])
        r_sb = sb("r_sb", [P, NT, D])
        agg = sb("agg", [P, 2, GT, D])
        node = sb("node", [P, 2, GT, D])
        node_t = sb("node_t", [D + 1, 2, GN])
        y = sb("y", [P, 2, GT, D])
        v = sb("v", [P, 2, GT, D])
        sq = sb("sq", [P, GT, D])
        moments = sb("moments", [P, GT, bn_dim])
        mean_var = sb("mean_var", [P, 2, GT, 2])
        rstd = sb("rstd", [P, 2, GT])
        shift = sb("shift", [P, 2, GT])
        eps = sb("eps", [P, 1])
        dev = sb("dev", [P, 2, GT])
        end_ix = sb("end_ix", [P, 2, GT], I32)
        ends = sb("ends", [P, NT + 2 * GT], I32)
        ids = sb("ids", [P, 2, TILES], I32)
        part = sb("part", [P, TILES], I32)
        lo = {k: sb(f"lo_{k}", [P, TILES], BF16) for k in ("dst", "src")}
        hi = {k: sb(f"hi_{k}", [P, TILES], BF16) for k in ("dst", "src")}
        flag = sb("flag", [P, TILES])
        keep_s = sb("keep_s", [P, TILES], BF16)
        keep_m = sb("keep_m", [P, TILES], BF16)
        deg = sb("deg", [P, NT])
        below = sb("below", [P, NT])
        tile_sum = sb("tile_sum", [P, NT])
        has = sb("has", [P, NT])
        norms = sb("norms", [P, 2, NT])
        roots = sb("roots", [P, 2, NT])
        dis, inn = norms[:, 0, :], norms[:, 1, :]
        dis2 = sb("dis2", [P, NT])
        outn = sb("outn", [P, NT])
        ident = sb("ident", [P, P])
        upper = sb("upper", [P, P])
        ones = sb("ones", [P, P])
        iota_i = sb("iota_i", [P, P], I32)
        iota_b = sb("iota_b", [P, P], BF16)
        zero_row = sb("zero_row", [1, D])
        falls = sb("falls", [P, 1])
        unordered = sb("unordered", [P, 1], I32)
        edge_row = sb("edge_row", [P, ROW])
        edge_col = sb("edge_col", [2 * DE32, P])
        dst_all = sb("dst_all", [P, P], I32)
        dst_all_f = sb("dst_all_f", [P, P])
        dst_f = sb("dst_f", [P, 1])
        lower = sb("lower", [P, P])
        one_lo = sb("one_lo", [P, P])
        one_lo_t = sb("one_lo_t", [P, P])
        one_hi = sb("one_hi", [P, NT])
        place = sb("place", [P, NT])
        rank = sb("rank", [P, 1])
        found = sb("found", [P, 1])
        to = sb("to", [P, 1], I32)
        minus_one = sb("minus_one", [1, 1], I32)
        W = {}
        loads = [("msg1", w_l0_msg1), ("root1", w_l0_root1), ("edge1", w_l0_edge1),
                 ("msg2", w_l0_msg2), ("root2", w_l0_root2), ("edge2", w_l0_edge2),
                 ("edge_in_b", b_edge_in), ("edge_out", w_edge_out),
                 ("self", w_self), ("neigh", w_neigh), ("l3", w_l3)]
        for name, ap in loads:
            W[name] = sb(f"w_{name}", list(ap.shape))

        banks = ctx.enter_context(nc.psum_tensor("banks", [P, 8, 512], F32))
        back_ps = [banks[:, b, 0:QT * D] for b in (0, 1)]
        w_ps = [banks[:, b, 0:QT * D] for b in (2, 3)]
        turn_ps = [banks[0:D, b, :] for b in (4, 5)]
        hid_ps = [banks[0:D, b, :] for b in (6, 7)]
        hist_ps = banks[:, 6, 0:NT]
        pre_ps = banks[:, 7, 0:2 * NT]
        falls_ps = banks[:, 7, 0:1]
        one_lo_ps, edge_col_ps = banks[:, 2, 0:P], banks[0:2 * DE32, 2, 0:P]
        place_ps, count_ps = banks[:, 3, 0:NT], banks[:, 4, 0:NT]
        node_turn_ps = banks[0:D, 2:4, :].rearrange("p b c -> p (b c)")[:, 0:GN]
        y_ps = [banks[:, b, 0:GF] for b in (4, 5)]
        r_ps = [banks[:, b, 0:GF] for b in (6, 7)]

        s_falls = sem("s_falls")
        s_falls_sum = sem("s_falls_sum")
        s_order = sem("s_order")
        o_hot = sem("o_hot")
        o_hist = sem("o_hist")
        o_hist_all = sem("o_hist_all")
        o_prefix = sem("o_prefix")
        o_tile = sem("o_tile")
        o_load = sem("o_load")
        o_one = sem("o_one")
        o_turn = sem("o_turn")
        o_turned = sem("o_turned")
        o_found = sem("o_found")
        o_to = sem("o_to")
        o_put = sem("o_put")
        o_row = sem("o_row")
        o_col_ps = sem("o_col_ps")
        o_col = sem("o_col")
        o_ids = sem("o_ids")
        o_out = sem("o_out")
        s_msg1 = sem("s_msg1")
        s_first_weights = sem("s_first_weights")
        s_weights = sem("s_weights")
        s_ids = sem("s_ids")
        s_seq = sem("s_seq")
        s_const = sem("s_const")
        s_keep_made = sem("s_keep_made")
        s_keep_out = sem("s_keep_out")
        s_x = sem("s_x")
        s_ones_row = sem("s_ones_row")
        s_x_t = [sem(f"s_x_t{n}") for n in range(GPAIRS)]
        s_ix = [sem(f"s_ix{b}") for b in (0, 1)]
        s_ea = [sem(f"s_ea{b}") for b in (0, 1)]
        s_keep = [sem(f"s_keep{b}") for b in (0, 1)]
        s_gath = [sem(f"s_gath{k}") for k in range(8)]
        s_hid_ps = sem("s_hid_ps")
        s_hid = sem("s_hid")
        s_part = [sem(f"s_part{n}") for n in range(3)]
        s_rest = [sem(f"s_rest{n}") for n in range(2)]
        s_w_in = sem("s_w_in")
        s_w_parts = sem("s_w_parts")
        s_w = sem("s_w")
        s_msg = sem("s_msg")
        s_turn = sem("s_turn")
        s_scan = sem("s_scan")
        s_back = sem("s_back")
        s_evac = sem("s_evac")
        s_rows = [sem(f"s_rows{b}") for b in (0, 1)]
        s_passed = sem("s_passed")
        s_hot = sem("s_hot")
        s_hist = sem("s_hist")
        s_deg = sem("s_deg")
        s_prefix = sem("s_prefix")
        s_ends = sem("s_ends")
        s_roots = sem("s_roots")
        def in_parts(name, *which):
            return {n: sem(f"{name}_{n}") for n in which}

        s_end_ix = in_parts("s_end_ix", 1, 2, 3, 4, 5, 6)
        s_agg = {n: [sem(f"s_agg{b}_{n}") for b in (0, 1)] for n in (1, 2, 3, 4, 5, 6)}
        s_agg_used = in_parts("s_agg_used", 1, 2, 4, 5)
        s_node = in_parts("s_node", 1, 2, 6)
        s_nturn = in_parts("s_nturn", 1, 2, 3, 6)
        s_nt = in_parts("s_nt", 1, 2, 3, 6)
        s_mm = in_parts("s_mm", 0, 1, 2, 3, 6)
        s_copied = in_parts("s_copied", 0, 1, 2, 3, 6)
        s_y = in_parts("s_y", 0, 1, 3, 4, 5, 6)
        s_var = in_parts("s_var", 2, 3, 5, 6)
        s_dev = in_parts("s_dev", 2, 3, 5, 6)
        s_rstd = in_parts("s_rstd", 2, 3, 5, 6)
        s_table = {n: [sem(f"s_table{b}_{n}") for b in (0, 1)] for n in range(PASSES + 1)}

        def x_columns(g, groups=1, k=D):
            to, at = (scan, g) if g < 6 else (back, g - 6)
            return to[0:k, :, :].rearrange("p b e -> p (b e)")[:, at * GN:(at + groups) * GN]

        def over_pairs(eng, pair):
            pair(0, True, False)
            with eng.Fori(1, PAIRS - 1) as i:
                pair(i, False, False)
            pair(PAIRS - 1, False, True)

        def over_groups(eng, *stages):
            def step(i, b, known):
                for stage, lag in stages:
                    g = 2 * i + b - lag if known else None
                    if not known or 0 <= g < GROUPS:
                        stage(i + (b - lag) // 2, (b - lag) % 2, known and g < 2)
            for s in range(4):
                step(s // 2, s % 2, True)
            with eng.Fori(2, GPAIRS) as i:
                step(i, 0, False)
                step(i, 1, False)
            for s in range(GROUPS, GROUPS + max(lag for _, lag in stages)):
                step(s // 2, s % 2, True)

        def under(i, k, n):
            return type(i) is int and 8 * i + k < n

        def of_group(table, i, b):
            return table[:, bass.ds((2 * i + b) * GT, GT), :]

        def spread(table, i, b):
            return table[:, bass.ds((2 * i + b) * GT, GT)].unsqueeze(2).to_broadcast([P, GT, D])

        block = ctx.enter_context(nc.Block())

        @block.sync
        def _(sp):
            sp.dma_start(W["msg1"][:, :], w_l0_msg1).then_inc(s_msg1, 16)
            for n in range(GPAIRS):
                sp.dma_start(x_columns(2 * n, 2), x_t[:, 2 * n * GN:2 * (n + 1) * GN]).then_inc(s_x_t[n], 16)
            sp.dma_start(W["root1"][:, :], w_l0_root1).then_inc(s_first_weights, 16)
            sp.dma_start(W["edge1"][:, :], w_l0_edge1).then_inc(s_first_weights, 16)

            def store_y(n, table):
                def group(i, b, first):
                    sp.wait_ge(s_y[n], 2 * i + b + 1)
                    sp.dma_start(of_group(table, i, b), y[:, b, :, :]).then_inc(s_table[n][b], 16)
                return group

            for g in range(GROUPS):
                sp.wait_ge(s_y[0], g + 1)
                sp.dma_start(of_group(tables_v[0], 0, g), of_group(x_sb, 0, g)).then_inc(s_table[0][g % 2], 16)
            sp.wait_ge(s_order, 1)
            out_of_order = sp.value_load(unordered[0:1, 0:1], min_val=0, max_val=1)
            with sp.If(out_of_order > 0):
                with sp.Fori(0, TILES) as t:
                    sp.wait_ge(o_tile, t + 1)
                    sp.sem_inc(s_passed, 1)
                    tile = bass.ds(P * t, P)
                    sp.dma_start(edge_row[:, 0:DE32], ea32_rows[tile, :]).then_inc(o_load, 16)
                    sp.dma_start(edge_row[:, DE32:2 * DE32], ea17_rows[tile, :]).then_inc(o_load, 16)
                    sp.dma_start(dst_all[:, :], dst_seq[0:1, tile].to_broadcast([P, P])).then_inc(o_load, 16)
                sp.wait_ge(o_tile, TILES + 1)
                sp.dma_start(ordered_dst[0:1].unsqueeze(0), minus_one[:, :]).then_inc(o_out, 16)
                with sp.Fori(0, TILES) as t:
                    sp.wait_ge(o_out, 16 + 48 * t)
                    sp.sem_inc(s_passed, 1)
                    sp.wait_ge(o_ids, t + 1)
                    sp.sem_inc(s_passed, 1)
                    tile = bass.ds(P * t, P)
                    sp.dma_start(edge_row[:, :], ordered[tile, :]).then_inc(o_row, 16)
                    sp.wait_ge(o_col, t + 1)
                    sp.sem_inc(s_passed, 1)
                    sp.dma_start(ordered_ea[EDGE32][:, tile], edge_col[0:DE32, :]).then_inc(o_out, 16)
                    sp.dma_start(ordered_ea[EDGE17][:, tile], edge_col[DE32:2 * DE32, :]).then_inc(o_out, 16)
                    sp.dma_start(ordered_dst[bass.ds(P * t + 1, P)].unsqueeze(1),
                                 edge_row[:, DST_AT:DST_AT + 1].bitcast(I32)).then_inc(o_out, 16)
                sp.wait_ge(o_ids, TILES + 1)
                sp.dma_start(ordered_src, ids[:, 1, :]).then_inc(o_out, 16)
                sp.wait_ge(o_out, 16 + 48 * TILES + 16)
                sp.dma_start(part[:, :], ordered_dst[1:1 + EP].rearrange("(p n) -> p n", p=P)).then_inc(s_seq, 16)
                sp.dma_start(flag[:, :].bitcast(I32), ordered_dst[0:EP].rearrange("(p n) -> p n", p=P)).then_inc(s_seq, 16)

            def load_edges(to, given, ordered_here, done):
                sp.sem_inc(s_passed, 1)
                with sp.If(out_of_order > 0):
                    sp.dma_start(to, ordered_here).then_inc(done, 16)
                with sp.Else():
                    sp.dma_start(to, given).then_inc(done, 16)

            for p in range(PASSES):
                keep_d = keep_max_d if IS_MAX[p] else keep_sum_d

                def loads_of_pair(i, first, last):
                    for b in (0, 1):
                        q = 8 * i + 4 * b
                        at = bass.ds(CHUNK * (2 * i + b), CHUNK)
                        if KIND[p] == EDGE17:
                            if not first:
                                sp.wait_ge(s_part[2], 2 * i + b - 1)
                            for to in COPIES:
                                load_edges(ea[to:to + DE32, b, :], ea17_t[:, at], ordered_ea[EDGE17][:, at], s_ea[b])
                        if not first:
                            for k in range(4):
                                sp.wait_ge(s_gath[4 * b + k], 16 * QT * (PAIRS * p + i))
                        tiles = bass.ds(CT * (2 * i + b), CT)
                        load_edges(src_ix[:, b, :], src_t[:, tiles], ordered_src[:, tiles], s_ix[b])
                        if KIND[p] == EDGE32:
                            if not first:
                                sp.wait_ge(s_w, QUARTERS * p + q - 4)
                            load_edges(ea[0:DE32, b, :], ea32_t[:, at], ordered_ea[EDGE32][:, at], s_ea[b])
                        if not first:
                            sp.wait_ge(s_scan, QUARTERS * p + q - 4)
                            sp.sem_inc(s_passed, 1)
                        if p == 0 and first and b == 0:
                            sp.wait_ge(s_keep_out, 32)
                        sp.dma_start(keep[:, b, :], keep_d[0:1, at].to_broadcast([D, CHUNK])).then_inc(s_keep[b], 16)

                over_pairs(sp, loads_of_pair)

                n = p + 1
                if p == 0:
                    over_groups(sp, (store_y(n, tables_v[1]), 0))
                elif p == 1:
                    def store_node(i, b, first):
                        sp.wait_ge(s_node[n], 2 * i + b + 1)
                        sp.dma_start(of_group(tables_v[2], i, b), node[:, b, :, :]).then_inc(s_table[n][b], 16)
                    over_groups(sp, (store_node, 0))
                elif p < 5:
                    def store_r(i, b, first):
                        sp.wait_ge(s_y[n], 2 * i + b + 1)
                        sp.dma_start(of_group(tables_v[p + 1], i, b), of_group(r_sb, i, b)).then_inc(s_table[n][b], 16)
                    over_groups(sp, (store_r, 0))
                else:
                    over_groups(sp, (store_y(n, out_v), 0))
            for b in (0, 1):
                sp.wait_ge(s_table[PASSES][b], 16 * GPAIRS)

        @block.gpsimd
        def _(pool):
            pool.memset(ident[:, :], 1.0)
            pool.memset(upper[:, :], 1.0)
            pool.memset(ones[:, :], 1.0)
            pool.memset(zero_row[:, :], 0.0)
            pool.iota(iota_i[:, :], [[1, P]], base=0, channel_multiplier=0).then_inc(s_const, 1)
            pool.drain()
            pool.tensor_copy(iota_b[:, :], iota_i[:, :]).then_inc(s_const, 1)
            pool.affine_select(out=ident[:, :], in_=ident[:, :], compare_op=ALU.is_equal, fill=0.0, base=0,
                               pattern=[[-1, P]], channel_multiplier=1).then_inc(s_const, 1)
            pool.affine_select(out=upper[:, :], in_=upper[:, :], compare_op=ALU.is_ge, fill=0.0, base=0,
                               pattern=[[1, P]], channel_multiplier=-1).then_inc(s_const, 1)

            pool.wait_ge(s_order, 1)
            out_of_order = pool.value_load(unordered[0:1, 0:1], min_val=0, max_val=1)
            with pool.If(out_of_order > 0):
                pool.memset(minus_one[:, :], -1)
                pool.drain()
                pool.sem_inc(o_tile, 1)
                with pool.Fori(0, TILES) as t:
                    pool.wait_ge(o_to, t + 1)
                    pool.sem_inc(s_passed, 1)
                    pool.indirect_dma_start(ordered[:, :], bass.IndirectOffsetOnAxis(ap=to[:, 0:1], axis=0),
                                            edge_row[:, :], None).then_inc(o_put, 16)
                    pool.wait_ge(o_put, 16 * t + 16)
                    pool.sem_inc(o_tile, 1)

            for p in range(PASSES):
                for b in (0, 1):
                    pool.wait_ge(s_table[p][b], 16 * GPAIRS)

                def gather_pair(i, first, last):
                    for b in (0, 1):
                        pool.wait_ge(s_ix[b], 16 * (PAIRS * p + i + 1))
                        for k in range(4):
                            if not first:
                                q = QUARTERS * p + 8 * i + 4 * b + k - 7
                                pool.wait_ge(s_turn if KIND[p] == PLAIN else s_msg, q)
                            pool.sem_inc(s_passed, 1)
                            for t in range(QT * k, QT * k + QT):
                                pool.indirect_dma_start(
                                    gath[:, b, t, :], None, tables[p][:, :],
                                    bass.IndirectOffsetOnAxis(ap=src_ix[:, b, t:t + 1], axis=0),
                                ).then_inc(s_gath[4 * b + k], 16)

                over_pairs(pool, gather_pair)

                n = p + 1
                for b in (0, 1):
                    pool.wait_ge(s_rows[b], 16 * (STORES[b] * (p + 1) + b))

                def gather_ends(i, b, first):
                    if not first:
                        pool.wait_ge({2: s_nturn, 5: s_node}.get(p, s_agg_used)[n], 2 * i + b - 1)
                    pool.wait_ge(s_end_ix[n], 2 * i + b + 1)
                    pool.sem_inc(s_passed, 1)
                    for t in range(GT):
                        pool.indirect_dma_start(
                            agg[:, b, t, :], None, rows[:, :],
                            bass.IndirectOffsetOnAxis(ap=end_ix[:, b, t:t + 1], axis=0),
                        ).then_inc(s_agg[n][b], 16)

                over_groups(pool, (gather_ends, 0))

        @block.tensor
        def _(pe):
            pe.wait_ge(s_const, 5)
            pe.wait_ge(s_msg1, 16)

            def products(done, to, columns, w):
                for t in range(GT):
                    m = pe.matmul(to[:, t * D:(t + 1) * D], columns[:, t * P:(t + 1) * P], W[w][0:columns.shape[0], :],
                                  start=True, stop=True)
                m.then_inc(done, 1)

            for g in range(GROUPS):
                if g % 2 == 0:
                    pe.wait_ge(s_x_t[g // 2], 16)
                if g >= 2:
                    pe.wait_ge(s_y[0], g - 1)
                products(s_mm[0], y_ps[g % 2], x_columns(g), "msg1")
                if g == 4:
                    pe.wait_ge(s_falls, 1)
                    pe.matmul(falls_ps, ones[:, :], falls[:, :], start=True, stop=True).then_inc(s_falls_sum, 1)
            pe.wait_ge(s_order, 1)
            out_of_order = pe.value_load(unordered[0:1, 0:1], min_val=0, max_val=1)
            with pe.If(out_of_order > 0):
                pe.wait_ge(s_y[0], GROUPS)
                with pe.Fori(0, QUARTERS) as q:
                    pe.wait_ge(o_hot, q + 1)
                    for t in range(QT):
                        m = pe.matmul(hist_ps, hot_lo[:, 0, t, :], hot_hi[:, 0, t, :], start=t == 0, stop=t == QT - 1)
                    m.then_inc(o_hist, 1)
                pe.wait_ge(o_hist_all, 1)
                pe.matmul(pre_ps[:, 0:NT], upper[:, :], place[:, :], start=True, stop=True)
                pe.matmul(pre_ps[:, NT:2 * NT], ones[:, :], place[:, :], start=True, stop=True).then_inc(o_prefix, 1)
                with pe.Fori(0, TILES) as t:
                    pe.wait_ge(o_one, t + 1)
                    pe.transpose(one_lo_ps, one_lo[:, :], ident[:, :]).then_inc(o_turn, 1)
                    pe.matmul(count_ps, one_lo[:, :], one_hi[:, :], start=True, stop=True)
                    pe.wait_ge(o_turned, t + 1)
                    pe.matmul(place_ps, one_lo_t[:, :], place[:, :], start=True, stop=True).then_inc(o_found, 1)
                with pe.Fori(0, TILES) as t:
                    pe.wait_ge(o_row, 16 * t + 16)
                    pe.sem_inc(s_passed, 1)
                    pe.transpose(edge_col_ps, edge_row[:, 0:2 * DE32], ident[:, :]).then_inc(o_col_ps, 1)
            pe.wait_ge(s_first_weights, 32)
            pe.wait_ge(s_ones_row, 1)
            for g in range(GROUPS):
                if g >= 2:
                    pe.wait_ge(s_copied[0], g - 1)
                products(s_mm[0], r_ps[g % 2], x_columns(g, k=D + 1), "root1")

            def columns_of(w, b):
                return node_t[0:W[w].shape[0], b, :]

            for p in range(PASSES):
                base = QUARTERS * p
                if p < 3:
                    pe.wait_ge(s_copied[p], GROUPS)

                def hidden(i, k):
                    b, at = k // 4, k % 4 * Q
                    if at == 0:
                        pe.wait_ge(s_part[2], 2 * i + b + 1)
                    if not under(i, k, 2):
                        pe.wait_ge(s_hid, 8 * i + k - 1)
                    for n in range(3):
                        m = pe.matmul(hid_ps[k % 2], w_parts[n][:, :], parts[:, b, at:at + Q],
                                      start=n == 0, stop=n == 2)
                    m.then_inc(s_hid_ps, 1)

                def edge_rows(i, k):
                    b, at = k // 4, k % 4 * Q
                    if not under(i, k, 2):
                        pe.wait_ge(s_msg, base + 8 * i + k - 1)
                    if KIND[p] == EDGE17:
                        pe.wait_ge(s_hid, 8 * i + k + 1)
                    elif at == 0:
                        pe.wait_ge(s_ea[b], 16 * (PAIRS * p + i + 1))
                    for t in range(QT):
                        if KIND[p] == EDGE17:
                            lhs, w = hid[:, k % 2, t * P:(t + 1) * P], W["edge_out"]
                        else:
                            lhs, w = ea[0:DE32, b, at + t * P:at + (t + 1) * P], W["edge1" if p == 0 else "edge2"]
                        m = pe.matmul(w_ps[k % 2][:, t * D:(t + 1) * D], lhs, w[:, :], start=True, stop=True)
                    m.then_inc(s_w, 1)

                def turn(i, k):
                    if KIND[p] == PLAIN:
                        pe.wait_ge(s_gath[k], 16 * QT * (PAIRS * p + i + 1))
                    else:
                        pe.wait_ge(s_msg, base + 8 * i + k + 1)
                    if not under(i, k, 2):
                        pe.wait_ge(s_scan, base + 8 * i + k - 1)
                    for t in range(QT):
                        if KIND[p] == PLAIN:
                            rows_in = gath[:, k // 4, QT * (k % 4) + t, :]
                        else:
                            rows_in = msg[:, k % 2, t * D:(t + 1) * D]
                        m = pe.transpose(turn_ps[k % 2][:, t * P:(t + 1) * P], rows_in, ident[:, :])
                    m.then_inc(s_turn, 1)

                def turn_back(i, k, first):
                    if first and k < LAG:
                        return
                    g8 = (k - LAG) % 8
                    b, g = g8 // 4, g8 % 4
                    pe.wait_ge(s_scan, base + 8 * i + k - LAG + 1)
                    if not (first and k < LAG + 2):
                        pe.wait_ge(s_evac, base + 8 * i + k - LAG - 1)
                    for t in range(QT):
                        m = pe.transpose(back_ps[g8 % 2][:, t * D:(t + 1) * D],
                                         scan[0:D, b, Q * g + t:Q * (g + 1):QT], ident[0:D, 0:D])
                    m.then_inc(s_back, 1)

                hist_base = QUARTERS * (p // 3)

                def count(i, k, first, last):
                    if p not in HISTOGRAM or (first and k < 2):
                        return
                    h = k % 2
                    pe.wait_ge(s_hot, hist_base + 8 * i + k - 1)
                    for t in range(QT):
                        m = pe.matmul(hist_ps, hot_lo[:, h, t, :], hot_hi[:, h, t, :],
                                      start=first and k == 2 and t == 0, stop=last and k == 1 and t == QT - 1,
                                      skip_group_check=True)
                    m.then_inc(s_hist, 1)

                if KIND[p] == EDGE17:
                    pe.wait_ge(s_w_parts, 1)
                    hidden(0, 0)
                    hidden(0, 1)
                if KIND[p] != PLAIN:
                    edge_rows(0, 0)

                def pair(i, first, last):
                    for k in range(8):
                        if KIND[p] == EDGE17 and not (last and k > 5):
                            hidden(i + (k + 2) // 8, (k + 2) % 8)
                        if KIND[p] != PLAIN and not (last and k == 7):
                            edge_rows(i + (k + 1) // 8, (k + 1) % 8)
                        turn_back(i, k, first)
                        count(i, k, first, False)
                        turn(i, k)

                over_pairs(pe, pair)
                for k in range(LAG):
                    if k < 2:
                        count(PAIRS, k, False, True)
                    turn_back(PAIRS, k, False)

                n = p + 1
                if p == 0:
                    pe.wait_ge(s_weights, 16 * (len(loads) - 3))
                    pe.wait_ge(s_deg, 1)
                    pe.matmul(pre_ps[:, 0:NT], upper[:, :], deg[:, :], start=True, stop=True)
                    pe.matmul(pre_ps[:, NT:2 * NT], ones[:, :], deg[:, :], start=True, stop=True).then_inc(s_prefix, 1)
                    pe.wait_ge(s_ends, 1)

                def turn_nodes(i, b, first):
                    if p == 2:
                        pe.wait_ge(s_agg[n][b], 16 * GT * (i + 1))
                    else:
                        pe.wait_ge(s_node[n], 2 * i + b + 1)
                    if not (first and b == 0):
                        pe.wait_ge(s_nt[n], 2 * i + b)
                    for t in range(GT):
                        m = pe.transpose(node_turn_ps[:, t * P:(t + 1) * P],
                                         agg[:, b, t, :] if p == 2 else node[:, b, t, :], ident[:, :])
                    m.then_inc(s_nturn[n], 1)

                def multiply_y(i, b, first):
                    w = {0: "msg2", 2: "neigh", 5: "l3"}[p]
                    pe.wait_ge(s_nt[n], 2 * i + b + 1)
                    if not first:
                        pe.wait_ge((s_y if p == 0 else s_copied)[n], 2 * i + b - 1)
                    products(s_mm[n], y_ps[b], columns_of(w, b), w)

                def multiply_r(i, b, first):
                    w = {0: "root2", 1: "self"}[p]
                    if p == 1:
                        pe.wait_ge(s_nt[n], 2 * i + b + 1)
                    if not first:
                        pe.wait_ge(s_copied[n], 2 * i + b - 1)
                    products(s_mm[n], r_ps[b], columns_of(w, b), w)

                stages = {0: [(turn_nodes, 0), (multiply_r, 1), (multiply_y, 0)],
                          1: [(multiply_r, 2), (turn_nodes, 0)],
                          2: [(turn_nodes, 0), (multiply_y, 0)],
                          5: [(turn_nodes, 0), (multiply_y, 0)]}.get(p)
                if stages:
                    over_groups(pe, *stages)

        @block.scalar
        def _(act):
            act.dma_start(part[:, :], dst_now).then_inc(s_seq, 16)
            act.dma_start(flag[:, :].bitcast(I32), dst_before).then_inc(s_seq, 16)

            for g in range(GROUPS):
                act.wait_ge(s_mm[0], g + 1)
                act.activation(of_group(x_sb, 0, g), y_ps[g % 2].rearrange("p (t f) -> p t f", f=D), ACT.Copy)\
                   .then_inc(s_y[0], 1)
            act.dma_start(ids[:, 0, :], dst_t).then_inc(s_ids, 16)
            act.dma_start(ids[:, 1, :], src_t).then_inc(s_ids, 16)
            act.wait_ge(s_order, 1)
            out_of_order = act.value_load(unordered[0:1, 0:1], min_val=0, max_val=1)
            with act.If(out_of_order > 0):
                with act.Fori(0, TILES) as t:
                    act.wait_ge(o_turn, t + 1)
                    act.activation(one_lo_t[:, :], one_lo_ps, ACT.Copy).then_inc(o_turned, 1)
                with act.Fori(0, TILES) as t:
                    act.wait_ge(o_col_ps, t + 1)
                    act.activation(edge_col[:, :], edge_col_ps, ACT.Copy).then_inc(o_col, 1)
            act.wait_ge(s_keep_made, 2)
            act.dma_start(keep_sum_d[0, :].rearrange("(p n) -> p n", p=P), keep_s[:, :]).then_inc(s_keep_out, 16)
            act.dma_start(keep_max_d[0, :].rearrange("(p n) -> p n", p=P), keep_m[:, :]).then_inc(s_keep_out, 16)
            for g in range(GROUPS):
                act.wait_ge(s_mm[0], GROUPS + g + 1)
                act.activation(of_group(r_sb, 0, g), r_ps[g % 2].rearrange("p (t f) -> p t f", f=D), ACT.Copy)\
                   .then_inc(s_copied[0], 1)
            for name, ap in loads:
                if name not in ("msg1", "root1", "edge1"):
                    act.dma_start(W[name][:, :], ap).then_inc(s_weights, 16)
            for to in COPIES:
                act.dma_start(w_in[to:to + DE32, :], w_edge_in).then_inc(s_w_in, 16)
            for b in (0, 1):
                act.wait_ge(s_table[0][b], 16 * GPAIRS)
            act.dma_start(x_sb[:, :, :], x_v).then_inc(s_x, 16)
            act.wait_ge(s_const, 5)
            act.dma_start(rows[EP:EP + 1, :], zero_row[:, :]).then_inc(s_rows[1], 16)

            for p in range(PASSES):
                base = QUARTERS * p

                def hidden_relu(i, k):
                    act.wait_ge(s_hid_ps, 8 * i + k + 1)
                    if not under(i, k, 2):
                        act.wait_ge(s_w, base + 8 * i + k - 1)
                    act.activation(hid[0:D, k % 2, :], hid_ps[k % 2], ACT.Relu, bias=W["edge_in_b"][:, 0:1])\
                       .then_inc(s_hid, 1)

                def evacuate(i, k, first):
                    if first and k < LAG:
                        return
                    g8 = (k - LAG) % 8
                    b, g = g8 // 4, g8 % 4
                    turn_i = i if k >= LAG else i - 1
                    if g == 0 and not (p == 0 and first):
                        act.wait_ge(s_rows[b], 16 * (STORES[b] * p + turn_i + b))
                    act.wait_ge(s_back, base + 8 * i + k - LAG + 1)
                    act.activation(back[:, b, g * QT * D:(g + 1) * QT * D], back_ps[g8 % 2], ACT.Copy).then_inc(s_evac, 1)
                    last_chunk = type(turn_i) is int and 2 * turn_i + b == 2 * PAIRS - 1
                    if g == 3 or last_chunk:
                        n = 1 if last_chunk else 4
                        act.wait_ge(s_evac, base + 8 * i + k - LAG + 1)
                        act.dma_start(rows_v[:, bass.ds(8 * turn_i + g8 - n + 1, n), :],
                                      back[:, b, (g - n + 1) * QT * D:(g + 1) * QT * D]
                                      .rearrange("p (q x) -> p q x", q=n)).then_inc(s_rows[b], 16)

                def take_part(i, b, n):
                    rows_in = slice(PART_AT[n], P)
                    if n == 0:
                        act.wait_ge(s_ea[b], 16 * (2 * PAIRS + len(COPIES) * (i + 1)))
                    else:
                        act.wait_ge(s_rest[n - 1], 2 * i + b + 1)
                    if n == 0 and not (type(i) is int and i == 0):
                        act.wait_ge(s_hid_ps, 8 * i + 4 * b - 4)
                    act.activation(parts[rows_in, b, :], ea[rows_in, b, :], ACT.Copy).then_inc(s_part[n], 1)

                if KIND[p] == EDGE17:
                    for n in range(3):
                        take_part(0, 0, n)
                    take_part(0, 1, 0)
                    take_part(0, 1, 1)
                    hidden_relu(0, 0)
                    hidden_relu(0, 1)

                def pair(i, first, last):
                    for k in range(8):
                        if KIND[p] == EDGE17 and not (last and k > 5):
                            hidden_relu(i + (k + 2) // 8, (k + 2) % 8)
                        evacuate(i, k, first)
                        if KIND[p] == EDGE17 and k in SPLIT_AT and not (last and k > 0):
                            turn, b, n = SPLIT_AT[k]
                            take_part(i + turn, b, n)

                over_pairs(act, pair)
                for k in range(LAG):
                    evacuate(PAIRS, k, False)

                n = p + 1
                if p == 0:
                    act.wait_ge(s_deg, 2)
                    act.activation(roots[:, :, :], norms[:, :, :], ACT.Sqrt).then_inc(s_roots, 1)
                if p == 3:
                    act.wait_ge(s_deg, 3)
                    act.activation(roots[:, 0, :], outn[:, :], ACT.Sqrt).then_inc(s_roots, 1)

                each = 2 if p == 0 else 1

                def take_turned(i, b, first):
                    act.wait_ge(s_nturn[n], 2 * i + b + 1)
                    if not first:
                        act.wait_ge(s_mm[n], each * (2 * i + b - 1))
                    act.activation(node_t[0:D, b, :], node_turn_ps, ACT.Copy).then_inc(s_nt[n], 1)

                def leave_y(i, b, first):
                    act.wait_ge(s_mm[n], each * (2 * i + b) + 1)
                    if not first:
                        act.wait_ge(s_table[n][b], 16 * i)
                    act.activation(y[:, b, :, :], y_ps[b].rearrange("p (t f) -> p t f", f=D), ACT.Copy)\
                       .then_inc(s_y[n], 1)

                def leave_r(i, b, first):
                    act.wait_ge(s_mm[n], each * (2 * i + b + 1))
                    act.activation(of_group(r_sb, i, b), r_ps[b].rearrange("p (t f) -> p t f", f=D), ACT.Copy)\
                       .then_inc(s_copied[n], 1)

                def deviation(i, b, first):
                    act.wait_ge(s_var[n], 2 * i + b + 1)
                    act.activation(dev[:, b, :], mean_var[:, b, :, 1], ACT.Sqrt, bias=eps[:, 0:1]).then_inc(s_dev[n], 1)

                def normalise(i, b, first):
                    def tile_of(table, t):
                        return table[:, bass.ds((2 * i + b) * GT + t, 1), :].rearrange("p a f -> p (a f)")
                    if p == 1 and not first:
                        act.wait_ge(s_nturn[n], 2 * i + b - 1)
                    if p in (1, 5) and not first:
                        act.wait_ge(s_table[n][b], 16 * i)
                    act.wait_ge(s_rstd[n], 2 * i + b + 1)
                    for t in range(GT):
                        to = {1: node[:, b, t, :], 5: y[:, b, t, :]}.get(p)
                        last = act.activation(tile_of(x_sb, t) if to is None else to, v[:, b, t, :], ACT.Identity,
                                              scale=rstd[:, b, t:t + 1], bias=shift[:, b, t:t + 1])
                    if p in (1, 5):
                        last.then_inc((s_node if p == 1 else s_y)[n], 1)
                        return
                    act.drain()
                    for t in range(GT):
                        factor = (dis if p == 2 else outn)[:, bass.ds((2 * i + b) * GT + t, 1)]
                        last = act.activation(tile_of(r_sb, t), tile_of(x_sb, t), ACT.Copy, scale=factor)
                    last.then_inc(s_y[n], 1)

                def keep_x(i, b, first):
                    act.wait_ge(s_node[n], 2 * i + b + 1)
                    act.activation(of_group(x_sb, i, b), node[:, b, :, :], ACT.Copy)

                stages = {0: [(take_turned, 0), (leave_r, 1), (leave_y, 0)],
                          1: [(take_turned, 1), (deviation, 0), (normalise, 0), (keep_x, 0), (leave_r, 2)],
                          2: [(take_turned, 0), (deviation, 1), (normalise, 1)],
                          4: [(deviation, 0), (normalise, 0)],
                          5: [(take_turned, 0), (deviation, 1), (normalise, 1)]}.get(p)
                if stages:
                    over_groups(act, *stages)

        @block.vector
        def _(ve):
            ve.memset(eps[:, :], EPS)
            ve.memset(ends[:, NT:], 0)
            ve.memset(w_in[DE32:COPIES[1], :], 0.0)
            ve.memset(hid[D:D + 1, :, :], 1.0)
            ve.memset(node_t[D:D + 1, :, :], 1.0).then_inc(s_const, 1)
            ve.wait_ge(s_seq, 32)
            ve.tensor_tensor(keep_s[:, :], part[:, :], flag[:, :].bitcast(I32), ALU.is_lt)
            ve.drain()
            ve.tensor_reduce(falls[:, :], keep_s[:, :], AX.X, ALU.max).then_inc(s_falls, 1)
            ve.memset(scan[D:D + 1, :, :], 1.0)
            ve.memset(back[D:D + 1, :, :], 1.0).then_inc(s_ones_row, 1)
            ve.wait_ge(s_falls_sum, 1)
            ve.tensor_scalar(unordered[:, :], falls_ps, 0.5, None, ALU.is_gt).then_inc(s_order, 1)

            def split_ids(n, k):
                tile_ids, place_ids = (x[:, :, :, :].rearrange("p b t f -> p (b t f)")[:, 0:TILES].bitcast(I32)
                                       for x in (v, node))
                ve.tensor_scalar(tile_ids, ids[:, n, :], 7, None, ALU.arith_shift_right)
                ve.tensor_scalar(place_ids, ids[:, n, :], P - 1, None, ALU.bitwise_and)
                ve.drain()
                ve.tensor_copy(hi[k][:, :], tile_ids)
                ve.tensor_copy(lo[k][:, :], place_ids)
                ve.drain()

            def quarter_hots(side, h, q):
                at = bass.ds(q * QT, QT)
                ve.tensor_tensor(hot_lo[:, h, :, :], lo[side][:, at].unsqueeze(2).to_broadcast([P, QT, P]),
                                 iota_b[:, :].unsqueeze(1).to_broadcast([P, QT, P]), ALU.is_equal)
                return ve.tensor_tensor(hot_hi[:, h, :, :], hi[side][:, at].unsqueeze(2).to_broadcast([P, QT, NT]),
                                        iota_b[:, 0:NT].unsqueeze(1).to_broadcast([P, QT, NT]), ALU.is_equal)

            def edges_below(prefix_ps):
                ve.tensor_copy(tile_sum[:, :], prefix_ps[:, NT:2 * NT])
                ve.drain()
                ve.tensor_tensor_scan(below[:, :], ones[:, 0:NT], tile_sum[:, :], 0.0, ALU.mult, ALU.add)
                ve.drain()
                ve.tensor_tensor(below[:, :], below[:, :], tile_sum[:, :], ALU.subtract)
                ve.drain()
                ve.tensor_tensor(below[:, :], below[:, :], prefix_ps[:, 0:NT], ALU.add)
                ve.drain()

            ve.wait_ge(s_const, 5)
            ve.wait_ge(s_order, 1)
            out_of_order = ve.value_load(unordered[0:1, 0:1], min_val=0, max_val=1)
            with ve.If(out_of_order > 0):
                ve.wait_ge(s_ids, 32)
                split_ids(0, "dst")
                ve.memset(place[:, :], 0.0)
                with ve.Fori(0, QUARTERS) as q:
                    quarter_hots("dst", 0, q).then_inc(o_hot, 1)
                    ve.wait_ge(o_hist, q + 1)
                    ve.tensor_tensor(place[:, :], place[:, :], hist_ps, ALU.add)
                    ve.drain()
                ve.tensor_scalar(lower[:, :], upper[:, :], -1.0, 1.0, ALU.mult, ALU.add).then_inc(o_hist_all, 1)
                ve.wait_ge(o_prefix, 1)
                edges_below(pre_ps)
                ve.tensor_tensor(place[:, :], below[:, :], place[:, :], ALU.subtract)
                ve.drain()
                with ve.Fori(0, TILES) as t:
                    ve.wait_ge(o_load, 48 * t + 48)
                    for n, at in ((0, DST_AT), (1, SRC_AT)):
                        ve.tensor_copy(edge_row[:, at:at + 1].bitcast(I32), ids[:, n, bass.ds(t, 1)])
                    ve.tensor_scalar(one_lo[:, :], iota_b[:, :], lo["dst"][:, bass.ds(t, 1)], None, ALU.is_equal)
                    ve.tensor_scalar(one_hi[:, :], iota_b[:, 0:NT], hi["dst"][:, bass.ds(t, 1)], None, ALU.is_equal)\
                      .then_inc(o_one, 1)
                    ve.tensor_copy(dst_all_f[:, :], dst_all[:, :])
                    ve.tensor_copy(dst_f[:, :], ids[:, 0, bass.ds(t, 1)])
                    ve.drain()
                    ve.scalar_tensor_tensor(dst_all_f[:, :], dst_all_f[:, :], dst_f[:, 0:1], lower[:, :],
                                            ALU.is_equal, ALU.mult)
                    ve.drain()
                    ve.tensor_reduce(rank[:, :], dst_all_f[:, :], AX.X, ALU.add)
                    ve.wait_ge(o_found, t + 1)
                    ve.tensor_tensor(below[:, :], place_ps, one_hi[:, :], ALU.mult)
                    ve.tensor_tensor(place[:, :], place[:, :], count_ps, ALU.add)
                    ve.drain()
                    ve.tensor_reduce(found[:, :], below[:, :], AX.X, ALU.add)
                    ve.drain()
                    ve.tensor_tensor(to[:, :], found[:, :], rank[:, :], ALU.add).then_inc(o_to, 1)
                ve.sem_inc(o_ids, 1)
                with ve.Fori(0, TILES) as t:
                    ve.wait_ge(o_row, 16 * t + 16)
                    ve.tensor_copy(ids[:, 0, bass.ds(t, 1)], edge_row[:, DST_AT:DST_AT + 1].bitcast(I32))
                    ve.tensor_copy(ids[:, 1, bass.ds(t, 1)], edge_row[:, SRC_AT:SRC_AT + 1].bitcast(I32)).then_inc(o_ids, 1)
                ve.wait_ge(s_seq, 64)

            ve.tensor_tensor(flag[:, :], part[:, :], flag[:, :].bitcast(I32), ALU.is_equal)
            ve.drain()
            ve.tensor_copy(keep_s[:, :], flag[:, :]).then_inc(s_keep_made, 1)
            ve.tensor_scalar(flag[:, :], flag[:, :], 2.0, -1.0, ALU.mult, ALU.add)
            ve.drain()
            ve.tensor_scalar(keep_m[:, :], flag[:, :], BIG, None, ALU.mult).then_inc(s_keep_made, 1)
            ve.wait_ge(s_ids, 32)
            ve.drain()
            split_ids(0, "dst")
            split_ids(1, "src")
            ve.wait_ge(s_const, 5)
            ve.drain()

            for p in range(PASSES):
                base = QUARTERS * p
                keep_op, take_op = (ALU.min, ALU.max) if IS_MAX[p] else (ALU.mult, ALU.add)

                def message(i, k):
                    ve.wait_ge(s_w, base + 8 * i + k + 1)
                    ve.wait_ge(s_gath[k], 16 * QT * (PAIRS * p + i + 1))
                    if not under(i, k, 2):
                        ve.wait_ge(s_turn, base + 8 * i + k - 1)
                    ve.tensor_tensor(msg[:, k % 2, :], w_ps[k % 2],
                                     gath[:, k // 4, QT * (k % 4):QT * (k % 4) + QT, :].rearrange("p t f -> p (t f)"),
                                     ALU.add if KIND[p] == EDGE32 else ALU.mult).then_inc(s_msg, 1)

                def leave_rest(i, b, n):
                    rows_in = slice(PART_AT[n + 1], P)
                    ve.wait_ge(s_part[n], 2 * i + b + 1)
                    ve.tensor_tensor(ea[rows_in, b, :], ea[rows_in, b, :], parts[rows_in, b, :], ALU.subtract)\
                      .then_inc(s_rest[n], 1)

                def scan_quarter(i, k, first):
                    b, at = k // 4, k % 4 * Q
                    if at == 0:
                        ve.wait_ge(s_keep[b], 16 * (PAIRS * p + i + 1))
                        if not first:
                            ve.wait_ge(s_back, base + 8 * i + k - 4)
                    if first and k == 0:
                        start = 0.0
                    else:
                        ve.wait_ge(s_scan, base + 8 * i + k)
                        start = scan[0:D, b, at - 1:at] if at else scan[0:D, 1 - b, CHUNK - 1:CHUNK]
                    ve.wait_ge(s_turn, base + 8 * i + k + 1)
                    ve.tensor_tensor_scan(scan[0:D, b, at:at + Q], keep[:, b, at:at + Q], turn_ps[k % 2],
                                          start, keep_op, take_op).then_inc(s_scan, 1)

                hist_base = QUARTERS * (p // 3)

                def one_hots(i, k, first):
                    if p not in HISTOGRAM:
                        return
                    side = HISTOGRAM[p]
                    h = k % 2
                    if not (first and k < 2):
                        ve.wait_ge(s_hist, hist_base + 8 * i + k - 1)
                    quarter_hots(side, h, 8 * i + k).then_inc(s_hot, 1)

                if p == 1:
                    ve.wait_ge(s_w_in, 16 * len(COPIES))
                    for n in range(3):
                        ve.drain()
                        ve.tensor_copy(w_parts[n][:, :], w_in[:, :])
                        ve.drain()
                        if n < 2:
                            ve.tensor_tensor(w_in[:, :], w_in[:, :], w_parts[n][:, :], ALU.subtract)
                    ve.memset(parts[DE32:COPIES[1], :, :], 0.0)
                    ve.memset(ea[DE32:COPIES[1], :, :], 0.0).then_inc(s_w_parts, 1)
                if KIND[p] == EDGE17:
                    leave_rest(0, 0, 0)
                    leave_rest(0, 0, 1)
                    leave_rest(0, 1, 0)
                    leave_rest(0, 1, 1)
                if KIND[p] != PLAIN:
                    message(0, 0)

                def pair(i, first, last):
                    for k in range(8):
                        if KIND[p] != PLAIN and not (last and k == 7):
                            message(i + (k + 1) // 8, (k + 1) % 8)
                        scan_quarter(i, k, first)
                        one_hots(i, k, first)
                        if KIND[p] == EDGE17 and k in SPLIT_AT and not (last and k > 0):
                            turn, b, n = SPLIT_AT[k]
                            if n < 2:
                                leave_rest(i + turn, b, n)

                over_pairs(ve, pair)

                def first_end_ix():
                    for b in (0, 1):
                        ve.tensor_copy(end_ix[:, b, :], ends[:, b * GT:(b + 1) * GT]).then_inc(s_end_ix[p + 1], 1)

                if p > 0:
                    first_end_ix()
                if p == 0:
                    ve.wait_ge(s_hist, QUARTERS)
                    ve.tensor_copy(deg[:, :], hist_ps).then_inc(s_deg, 1)
                    ve.drain()
                    ve.tensor_scalar(norms[:, 0, :], deg[:, :], 1.0, None, ALU.add)
                    ve.tensor_scalar(norms[:, 1, :], deg[:, :], 1.0, None, ALU.max).then_inc(s_deg, 1)
                    ve.tensor_scalar(has[:, :], deg[:, :], 0.5, None, ALU.is_gt)
                    ve.wait_ge(s_prefix, 1)
                    edges_below(pre_ps)
                    ve.scalar_tensor_tensor(below[:, :], below[:, :], -1.0 - EP, has[:, :], ALU.add, ALU.mult)
                    ve.drain()
                    ve.tensor_scalar(ends[:, 0:NT], below[:, :], float(EP), None, ALU.add).then_inc(s_ends, 1)
                    ve.drain()
                    first_end_ix()
                    ve.wait_ge(s_roots, 1)
                    ve.reciprocal(norms[:, :, :], roots[:, :, :])
                    ve.drain()
                    ve.tensor_tensor(dis2[:, :], dis, dis, ALU.mult)
                elif p == 3:
                    ve.wait_ge(s_hist, 2 * QUARTERS)
                    ve.tensor_scalar(outn[:, :], hist_ps, 1.0, None, ALU.max).then_inc(s_deg, 1)
                    ve.wait_ge(s_roots, 2)
                    ve.reciprocal(outn[:, :], roots[:, 0, :])
                    ve.drain()

                n = p + 1
                if p == 1:
                    ve.wait_ge(s_x, 16)
                if p < 3:
                    ve.wait_ge(s_copied[p], GROUPS)

                def end_ix_ahead(i, b, first):
                    ve.wait_ge(s_agg[n][b], 16 * GT * (i + 1))
                    ve.tensor_copy(end_ix[:, b, :], ends[:, bass.ds((2 * i + b + 2) * GT, GT)]).then_inc(s_end_ix[n], 1)

                def statistics(b):
                    ve.drain()
                    for t in range(GT):
                        ve.bn_stats(moments[:, t, :], v[:, b, t, :])
                    ve.drain()
                    for t in range(GT):
                        last = ve.bn_aggr(mean_var[:, b, t, :], moments[:, t, :])
                    last.then_inc(s_var[n], 1)

                def add_and_rectify(i, b, first):
                    ve.drain()
                    if p in NORMED and not first:
                        ve.wait_ge((s_node if p == 1 else s_y)[n], 2 * i + b - 1)
                    ve.wait_ge(s_agg[n][b], 16 * GT * (i + 1))
                    ve.tensor_tensor(v[:, b, :, :], agg[:, b, :, :], of_group(r_sb, i, b), ALU.add)\
                      .then_inc(s_agg_used[n], 1)
                    ve.drain()
                    if p == 0:
                        if not first:
                            ve.wait_ge(s_nturn[n], 2 * i + b - 1)
                        ve.scalar_tensor_tensor(node[:, b, :, :], v[:, b, :, :], SLOPE, v[:, b, :, :],
                                                ALU.mult, ALU.max).then_inc(s_node[n], 1)
                    else:
                        ve.scalar_tensor_tensor(sq[:, :, :], v[:, b, :, :], SLOPE, v[:, b, :, :], ALU.mult, ALU.max)
                        ve.drain()
                        ve.tensor_tensor(v[:, b, :, :], sq[:, :, :], of_group(x_sb, i, b), ALU.add)
                        statistics(b)

                def dense_sum(i, b, first):
                    products_in = y_ps[b].rearrange("p (t f) -> p t f", f=D)
                    ve.drain()
                    if p in NORMED and not first:
                        ve.wait_ge((s_node if p == 1 else s_y)[n], 2 * i + b - 1)
                    ve.wait_ge(s_mm[n], 2 * i + b + 1)
                    if p == 2:
                        ve.tensor_tensor(v[:, b, :, :], products_in, of_group(r_sb, i, b), ALU.add)\
                          .then_inc(s_copied[n], 1)
                        ve.drain()
                        ve.scalar_tensor_tensor(v[:, b, :, :], v[:, b, :, :], 0.0, of_group(x_sb, i, b), ALU.max, ALU.add)
                    else:
                        ve.tensor_tensor(v[:, b, :, :], products_in, of_group(x_sb, i, b), ALU.add)\
                          .then_inc(s_copied[n], 1)
                    statistics(b)

                def hop(i, b, first):
                    ve.drain()
                    if p in NORMED and not first:
                        ve.wait_ge((s_node if p == 1 else s_y)[n], 2 * i + b - 1)
                    ve.wait_ge(s_agg[n][b], 16 * GT * (i + 1))
                    ve.tensor_tensor(v[:, b, :, :], agg[:, b, :, :], of_group(r_sb, i, b), ALU.add)\
                      .then_inc(s_agg_used[n], 1)
                    ve.drain()
                    if p == 3:
                        ve.tensor_tensor(of_group(r_sb, i, b), v[:, b, :, :], spread(dis2, i, b), ALU.mult)\
                          .then_inc(s_y[n], 1)
                    else:
                        ve.tensor_tensor(v[:, b, :, :], v[:, b, :, :], spread(dis, i, b), ALU.mult)
                        ve.drain()
                        ve.tensor_tensor(v[:, b, :, :], v[:, b, :, :], of_group(x_sb, i, b), ALU.add)
                        statistics(b)

                def scale_in(i, b, first):
                    ve.wait_ge(s_agg[n][b], 16 * GT * (i + 1))
                    if not first:
                        ve.wait_ge(s_nturn[n], 2 * i + b - 1)
                    ve.tensor_tensor(node[:, b, :, :], agg[:, b, :, :], spread(inn, i, b), ALU.mult)\
                      .then_inc(s_node[n], 1)

                def factors(i, b, first):
                    ve.wait_ge(s_dev[n], 2 * i + b + 1)
                    ve.reciprocal(rstd[:, b, :], dev[:, b, :])
                    ve.drain()
                    ve.scalar_tensor_tensor(shift[:, b, :], mean_var[:, b, :, 0], -1.0, rstd[:, b, :],
                                            ALU.mult, ALU.mult).then_inc(s_rstd[n], 1)

                over_groups(ve, (end_ix_ahead, 0), *{0: [(add_and_rectify, 0)],
                                  1: [(add_and_rectify, 0), (factors, 0)],
                                  2: [(dense_sum, 0), (factors, 0)],
                                  3: [(hop, 0)],
                                  4: [(hop, 0), (factors, 0)],
                                  5: [(scale_in, 0), (dense_sum, 1), (factors, 1)]}[p])



def kernel(x, src, dst, edge_attr_17, edge_attr_32, L0_gnn_W1_msg, L0_gnn_W1_edge, L0_gnn_W1_root, L0_gnn_b1,
           L0_gnn_W2_msg, L0_gnn_W2_edge, L0_gnn_W2_root, L0_gnn_b2, L1_gnn_W1, L1_gnn_b1, L1_gnn_W2, L1_gnn_b2,
           L1_gnn_Ws, L1_gnn_bs, L1_gnn_Wn, L1_gnn_bn, L3_gnn_weight, L3_gnn_bias):
    import numpy as np
    import concourse.bacc as bacc
    from concourse.bass_utils import run_bass_kernel_spmd

    def padded(a, size, fill=0):
        a = np.asarray(a)
        return np.concatenate([a, np.full((size - a.shape[0],) + a.shape[1:], fill, a.dtype)])

    src, dst = padded(src, EP, NP - 1), padded(dst, EP, NP - 1)
    ea17, ea32 = padded(edge_attr_17, EP), padded(edge_attr_32, EP)
    x = padded(x, NP)
    before = np.concatenate([np.full((1,), -1, dst.dtype), dst[:-1]])
    inputs = {
        "x_nodes": x, "x_t": x.T,
        "src_t": src.reshape(TILES, P).T, "dst_t": dst.reshape(TILES, P).T,
        "dst_now": dst.reshape(P, TILES), "dst_before": before.reshape(P, TILES),
        "ea17_t": padded(ea17.T, DE32), "ea32_t": ea32.T, "ea17_rows": padded(ea17.T, DE32).T, "ea32_rows": ea32,
        "w_l0_msg1": L0_gnn_W1_msg, "w_l0_root1": np.vstack([L0_gnn_W1_root, L0_gnn_b1]), "w_l0_edge1": L0_gnn_W1_edge,
        "w_l0_msg2": L0_gnn_W2_msg, "w_l0_root2": np.vstack([L0_gnn_W2_root, L0_gnn_b2]), "w_l0_edge2": L0_gnn_W2_edge,
        "w_edge_in": padded(np.asarray(L1_gnn_W1).T, DE32), "b_edge_in": np.asarray(L1_gnn_b1)[:, None],
        "w_edge_out": np.vstack([np.asarray(L1_gnn_W2).T, L1_gnn_b2]),
        "w_self": np.vstack([np.asarray(L1_gnn_Ws).T, L1_gnn_bs]),
        "w_neigh": np.vstack([np.asarray(L1_gnn_Wn).T, L1_gnn_bn]),
        "w_l3": np.vstack([L3_gnn_weight, L3_gnn_bias]),
    }
    nc = bacc.Bacc("TRN2", target_bir_lowering=False, num_devices=1)
    arrays, args = {}, {}
    for name, a in inputs.items():
        a = np.ascontiguousarray(a)
        arrays[f"in_{name}"] = a
        args[name] = nc.dram_tensor(f"in_{name}", a.shape, mybir.dt.from_np(a.dtype), kind="ExternalInput").ap()
    args["out"] = nc.dram_tensor("out_x", (NP, D), F32, kind="ExternalOutput").ap()
    gnn_kernel(nc, **args)
    result = run_bass_kernel_spmd(nc, [arrays], core_ids=[0])
    return result.results[0]["out_x"][:N]
```
